# Optimizing a Trainium2 kernel written in Bass

```python
import numpy as np
import jax
import jax.numpy as jnp

def _softmax(x, axis=-1):
    return jax.nn.softmax(x, axis=axis)

def _gelu(x):
    return jax.nn.gelu(x, approximate=True)

def _silu(x):
    return jax.nn.silu(x)

def _sigmoid(x):
    return jax.nn.sigmoid(x)

def _layernorm(x, axis=-1, eps=1e-05):
    m = jnp.mean(x, axis=axis, keepdims=True)
    v = jnp.var(x, axis=axis, keepdims=True)
    return (x - m) / jnp.sqrt(v + eps)

def _scatter_add(tgt, idx, src, axis=0):
    return tgt.at[idx].add(src)

def _segment_sum(src, seg, n):
    return jax.ops.segment_sum(src, seg, n)
kernel_name = 'mk_macaron_d1_jaxref_r8_6863ba'

def setup_inputs(seed: int=0):
    np.random.seed(seed)
    _w = jnp.asarray

    def _L0_attn_setup():
        import jax, jax.numpy as jnp
        import numpy as np
        D_MODEL, H, DK, DV = (128, 16, 64, 64)
        key = jax.random.key(seed)
        ks = jax.random.split(key, 9)
        s = lambda fan_in: 1.0 / np.sqrt(fan_in)
        return {'x': jax.random.normal(ks[0], (2, 256, D_MODEL), dtype=jnp.float32), 'Wq': jax.random.uniform(ks[1], (D_MODEL, H * DK), jnp.float32, -s(D_MODEL), s(D_MODEL)), 'bq': jax.random.uniform(ks[2], (H * DK,), jnp.float32, -s(D_MODEL), s(D_MODEL)), 'Wk': jax.random.uniform(ks[3], (D_MODEL, DK), jnp.float32, -s(D_MODEL), s(D_MODEL)), 'bk': jax.random.uniform(ks[4], (DK,), jnp.float32, -s(D_MODEL), s(D_MODEL)), 'Wv': jax.random.uniform(ks[5], (D_MODEL, DV), jnp.float32, -s(D_MODEL), s(D_MODEL)), 'bv': jax.random.uniform(ks[6], (DV,), jnp.float32, -s(D_MODEL), s(D_MODEL)), 'Wo': jax.random.uniform(ks[7], (H * DV, D_MODEL), jnp.float32, -s(H * DV), s(H * DV)), 'bo': jax.random.uniform(ks[8], (D_MODEL,), jnp.float32, -s(H * DV), s(H * DV))}
    _L0_attn_in = _L0_attn_setup()

    def _L0_ffn_setup():
        import jax, jax.numpy as jnp
        import numpy as np
        K = 2
        key = jax.random.key(seed)
        ks = jax.random.split(key, 9)
        B, S, D, O, E = (4, 128, 128, 128, 8)
        sc = 0.02
        return {'x': jax.random.normal(ks[0], (B, S, D), dtype=jnp.float32), 'gate_w': jax.random.normal(ks[1], (D, E), dtype=jnp.float32) * sc, 'gate_b': jax.random.normal(ks[2], (E,), dtype=jnp.float32) * sc, 'w1': jax.random.normal(ks[3], (E, D, O), dtype=jnp.float32) * sc, 'b1': jax.random.normal(ks[4], (E, O), dtype=jnp.float32) * sc, 'w2': jax.random.normal(ks[5], (E, O, O), dtype=jnp.float32) * sc, 'b2': jax.random.normal(ks[6], (E, O), dtype=jnp.float32) * sc, 'w3': jax.random.normal(ks[7], (E, O, O), dtype=jnp.float32) * sc, 'b3': jax.random.normal(ks[8], (E, O), dtype=jnp.float32) * sc}
    _L0_ffn_in = _L0_ffn_setup()
    _d = {'L0_attn_x': _L0_attn_in['x'], 'L0_attn_Wq': _L0_attn_in['Wq'], 'L0_attn_bq': _L0_attn_in['bq'], 'L0_attn_Wk': _L0_attn_in['Wk'], 'L0_attn_bk': _L0_attn_in['bk'], 'L0_attn_Wv': _L0_attn_in['Wv'], 'L0_attn_bv': _L0_attn_in['bv'], 'L0_attn_Wo': _L0_attn_in['Wo'], 'L0_attn_bo': _L0_attn_in['bo'], 'L0_ffn_gate_w': _L0_ffn_in['gate_w'], 'L0_ffn_gate_b': _L0_ffn_in['gate_b'], 'L0_ffn_w1': _L0_ffn_in['w1'], 'L0_ffn_b1': _L0_ffn_in['b1'], 'L0_ffn_w2': _L0_ffn_in['w2'], 'L0_ffn_b2': _L0_ffn_in['b2'], 'L0_ffn_w3': _L0_ffn_in['w3'], 'L0_ffn_b3': _L0_ffn_in['b3']}
    _x0 = _d['L0_attn_x']
    _d['L0_attn_x'] = jax.random.normal(jax.random.fold_in(jax.random.key(seed), 1), (8, 512, 128), dtype=_x0.dtype)
    del _x0
    return _d

def reference(L0_attn_x, L0_attn_Wq, L0_attn_bq, L0_attn_Wk, L0_attn_bk, L0_attn_Wv, L0_attn_bv, L0_attn_Wo, L0_attn_bo, L0_ffn_gate_w, L0_ffn_gate_b, L0_ffn_w1, L0_ffn_b1, L0_ffn_w2, L0_ffn_b2, L0_ffn_w3, L0_ffn_b3):

    def _L0_attn_ref(x, Wq, bq, Wk, bk, Wv, bv, Wo, bo):
        import jax, jax.numpy as jnp
        import numpy as np
        D_MODEL, H, DK, DV = (128, 16, 64, 64)
        B, S, _ = x.shape
        q = (x @ Wq + bq).reshape(B, S, H, DK)
        k = x @ Wk + bk
        v = x @ Wv + bv
        scores = jnp.einsum('bshd,btd->bhst', q, k) / np.sqrt(DK).astype(x.dtype)
        w = jax.nn.softmax(scores, axis=-1)
        out = jnp.einsum('bhst,btd->bshd', w, v).reshape(B, S, H * DV)
        return out @ Wo + bo

    def _L0_ffn_ref(x, gate_w, gate_b, w1, b1, w2, b2, w3, b3):
        import jax, jax.numpy as jnp
        import numpy as np
        K = 2
        E = gate_w.shape[-1]
        logits = jnp.einsum('bsd,de->bse', x, gate_w) + gate_b
        probs = jax.nn.softmax(logits, axis=1)
        vals, idx = jax.lax.top_k(probs, K)
        h = jax.nn.relu(jnp.einsum('bsd,edo->ebso', x, w1) + b1[:, None, None, :])
        h = jax.nn.relu(jnp.einsum('ebso,eop->ebsp', h, w2) + b2[:, None, None, :])
        y = jax.nn.relu(jnp.einsum('ebso,eop->ebsp', h, w3) + b3[:, None, None, :])
        onehot = jax.nn.one_hot(idx, E, dtype=x.dtype)
        w_tok = jnp.einsum('bske,bsk->bse', onehot, vals)
        ind = onehot.max(axis=2)
        v = jnp.einsum('ebso,bse->eo', y, w_tok)
        out = jnp.einsum('bse,eo->bso', ind, v)
        return out
    x = L0_attn_x
    x = x + 0.5 * _L0_ffn_ref(_layernorm(x, axis=-1), L0_ffn_gate_w, L0_ffn_gate_b, L0_ffn_w1, L0_ffn_b1, L0_ffn_w2, L0_ffn_b2, L0_ffn_w3, L0_ffn_b3)
    x = x + _L0_attn_ref(_layernorm(x, axis=-1), L0_attn_Wq, L0_attn_bq, L0_attn_Wk, L0_attn_bk, L0_attn_Wv, L0_attn_bv, L0_attn_Wo, L0_attn_bo)
    x = x + 0.5 * _L0_ffn_ref(_layernorm(x, axis=-1), L0_ffn_gate_w, L0_ffn_gate_b, L0_ffn_w1, L0_ffn_b1, L0_ffn_w2, L0_ffn_b2, L0_ffn_w3, L0_ffn_b3)
    return x

_drawn_inputs = setup_inputs


def setup_inputs(seed=0):
    import zlib

    import numpy as np

    out = dict(_drawn_inputs(seed))
    spreads = {}
    factors = {'L0_attn_Wq': 4.941,
     'L0_attn_bq': 8.0,
     'L0_attn_Wk': 5.005,
     'L0_attn_bk': 64.0,
     'L0_attn_Wv': 2.986,
     'L0_attn_bo': 9.178,
     'L0_ffn_gate_b': 64.0,
     'L0_ffn_w1': 8.0,
     'L0_ffn_b1': 8.0,
     'L0_ffn_w2': 8.0,
     'L0_ffn_b2': 8.0,
     'L0_ffn_w3': 4.378,
     'L0_attn_bv': 4.343}
    for name, (base, spread) in spreads.items():
        noise = np.random.default_rng([zlib.crc32(name.encode()), seed]).standard_normal(out[name].shape)
        drawn = base * np.exp(spread * noise) if base else spread * noise
        out[name] = jnp.asarray(drawn.astype(out[name].dtype))
    for name, factor in factors.items():
        out[name] = (out[name] * factor).astype(out[name].dtype)
    return out
```

```python
from contextlib import ExitStack

import concourse.bass as bass
from concourse import mybir

F32 = mybir.dt.float32
F32R = mybir.dt.float32r
ALU = mybir.AluOpType
ACT = mybir.ActivationFunctionType
AX = mybir.AxisListType

P = 128
EPS = 1e-5


def wait(engine, semaphore, value):
    if isinstance(value, int) and value <= 0:
        return
    engine.wait_ge(semaphore, value)


def at(start, count=1):
    return slice(start, start + count) if isinstance(start, int) else bass.ds(start, count)


def macaron_kernel(nc, x, Wq, bq, Wk, bk, Wv, bv, Wo, bo, gate_w, gate_b, w1, b1, w2, b2, w3, b3, out):
    B, S, D = x.shape
    E = gate_w.shape[1]
    DK = Wk.shape[1]
    H = Wq.shape[1] // DK
    TPB = S // P
    NT = B * TPB
    NCH = H * DK // P
    SLOT = 32
    GROUPS = B // TPB
    QUADS = H // TPB
    HPQ = H // QUADS
    STEPS = HPQ * TPB
    SCALE = float(DK) ** -0.5
    assert D == P and E == 8 and DK == 64 and TPB == 4 and HPQ == 4

    with ExitStack() as ctx:
        def sb(name, shape, dt=F32):
            return ctx.enter_context(nc.sbuf_tensor(name, shape, dt))

        def bank(name):
            return ctx.enter_context(nc.psum_tensor(name, [P, 512], F32))

        def sem(name):
            return ctx.enter_context(nc.semaphore(name))

        xs = sb("xs", [P, NT, D])
        ident = sb("ident", [P, P])
        ones = sb("ones", [P, P])
        w1s, w2s, w3s = (sb(n, [P, E, P]) for n in ("w1s", "w2s", "w3s"))
        gws = sb("gws", [P, SLOT])
        wqs = sb("wqs", [P, H * DK])
        wks = sb("wks", [P, 2 * DK])
        wvs = sb("wvs", [P, DK])
        wos = sb("wos", [P, NCH, D])
        R_B1, R_B2, R_B3, R_BQ, R_BO, R_BK, ROWS = 0, E, 2 * E, 3 * E, 3 * E + NCH, 3 * E + NCH + 1, 3 * E + NCH + 2
        brow = sb("brow", [ROWS, P])
        bcol = sb("bcol", [P, ROWS])
        nb3 = sb("nb3", [P, E])
        gbc = sb("gbc", [P, 1])
        bvb = sb("bvb", [P, DK])
        prio = sb("prio", [P, E])
        stats = sb("stats", [P, NT, 6])
        mean = sb("mean", [P, NT])
        mdif = sb("mdif", [P, NT])
        var = sb("var", [P, NT])
        sq = sb("sq", [P, NT])
        std = sb("std", [P, NT])
        rstd = sb("rstd", [P, NT])
        xn = sb("xn", [P, 2, TPB, D])
        xnT = sb("xnT", [P, B, S])
        lgs = sb("lgs", [P, S])
        prs = sb("prs", [P, GROUPS, S])
        gst = sb("gst", [P, GROUPS, 4])
        pt = sb("pt", [P, NT, E])
        ta = sb("ta", [P, NT, E])
        tb = sb("tb", [P, NT, E])
        oh1 = sb("oh1", [P, NT, E])
        oh2 = sb("oh2", [P, NT, E])
        tm = sb("tm", [P, NT])
        wtok = sb("wtok", [P, NT, E])
        indp = sb("indp", [P, NT, SLOT])
        wp = sb("wp", [P, NT, SLOT])
        indT = sb("indT", [P, B, P])
        wT = sb("wT", [P, B, P])
        wb = sb("wb", [P, 2, E, S])
        h1 = sb("h1", [P, 2, S])
        h2 = sb("h2", [P, 2, S])
        vacc = sb("vacc", [P, E, B])
        wsum = sb("wsum", [P, E])
        vv = sb("vv", [P, 2, E])
        vrep = sb("vrep", [P, TPB, SLOT])
        VB = sb("VB", [P, TPB, D])
        wd = nc.dram_tensor("wd", [E, B, TPB, P], F32, kind="Internal").ap()
        QA = sb("QA", [P, QUADS, HPQ, S], F32R)
        QB = sb("QB", [DK + 1, QUADS, HPQ, S], F32R)
        KA = sb("KA", [P, S], F32R)
        KB = sb("KB", [DK + 1, S], F32R)
        KAn = sb("KAn", [P, S], F32R)
        KBn = sb("KBn", [DK, S], F32R)
        V = sb("V", [P, TPB, 2 * DK])
        Vn = sb("Vn", [P, TPB, DK])
        mx = sb("mx", [P, 2, STEPS])
        mT = sb("mT", [STEPS, P], F32R)
        rz = wb[0:DK, 1, 2, :]
        OT = xnT
        PT = wb[:, 0, 0:4, :]
        xaT = wb[:, 1, 0, :]
        yT = wb[:, 1, 1, :]

        psS = [bank("psS0"), bank("psS1")]
        psP = [bank("psP0"), bank("psP1")]
        psO = [bank("psO0"), bank("psO1")]
        X0, X1 = psX = [bank("psX0"), bank("psX1")]

        s_x = [sem(f"x_loaded{b}") for b in range(B)]
        s_wf = sem("ffn_weights_loaded")
        s_wa = sem("attn_weights_loaded")
        s_rows = sem("bias_rows_loaded")
        s_gb = sem("gate_bias_loaded")
        s_zero = sem("zeroed")
        s_id0 = sem("ident_zeroed")
        s_id = sem("ident_ready")
        s_bt = sem("bias_transposed")
        s_bc = sem("bias_columns")
        s_nb3 = sem("negated_b3")
        s_stats = sem("token_stats")
        s_ln = sem("ln_chain")
        s_var = sem("variance_ready")
        s_std = sem("std_ready")

        def ffn_sems(f):
            names = ("xn_done", "xn_transposed", "xnT_ready", "logits_done", "gate_chain", "logits_biased",
                     "gate_exp", "probs_ready", "probs_transposed", "picked", "picks_transposed", "indT_ready",
                     "wT_ready", "wsum_done", "wd_written", "wb_loaded", "l1_done", "l2_done", "l3_done",
                     "relu1_done", "relu2_done", "l3_bank_free", "v_chain", "v_ready", "v_transposed",
                     "VB_ready", "update_done", "x_updated")
            return {n: sem(f"f{f}_{n}") for n in names}

        F = [ffn_sems(0), ffn_sems(1)]
        s_axn = sem("a_xn_done")
        s_x0f, s_x0d = sem("x0_filled"), sem("x0_drained")
        s_x1f, s_x1d = sem("x1_filled"), sem("x1_drained")
        s_khi = sem("k_high")
        s_sw = sem("switched")
        s_qhi = sem("q_high")
        s_qdup = sem("q_high_copied")
        s_s, s_max = sem("scores_for_max"), sem("max_done")
        s_mrow = sem("max_row_placed")
        s_st, s_exp, s_pv = sem("scoresT_done"), sem("exp_done"), sem("pv_done")
        s_rz, s_on = sem("reciprocal_done"), sem("head_normalised")
        s_out = sem("out_written")

        block = ctx.enter_context(nc.Block())

        X0_START, X0_PER_B = 6, 10
        X1_START, X1_PER_B = 2, 7

        def x0_use(b, idx):
            return X0_START + X0_PER_B * b + idx

        def x1_use(b, idx):
            return X1_START - 1 + X1_PER_B * b + idx

        def x0_of_q(b, i, ch):
            if i >= 2:
                return x0_use(b, 2 * (i - 2) + ch)
            if isinstance(b, int) and b == 0:
                return 2 + 2 * i + ch
            return x0_use(b - 1, 6 + 2 * i + ch)

        def x0_of_k(b):
            return 0 if isinstance(b, int) and b == 0 else x0_use(b - 1, 4)

        def x0_of_v(b):
            return 1 if isinstance(b, int) and b == 0 else x0_use(b - 1, 5)

        def x1_of_xt(b):
            return 0 if isinstance(b, int) and b == 0 else x1_use(b - 1, 2)

        def x1_of_mt(b, i):
            if i == 0:
                return 1 if isinstance(b, int) and b == 0 else x1_use(b - 1, 5)
            last = isinstance(b, int) and b == B - 1
            return x1_use(b, {1: 1, 2: 2 if last else 3, 3: 3 if last else 4}[i])

        def x1_of_op(b):
            return x1_use(b, 4 if isinstance(b, int) and b == B - 1 else 6)

        def x1_of_yt(b):
            return x1_use(b, 5) if isinstance(b, int) and b == B - 1 else x1_use(b + 1, 0)

        X1_ALL = X1_START - 1 + X1_PER_B * (B - 1) + 6

        def side_steps(i, n, has_prev, has_next):
            todo = []
            if i == 0 and n == 3 and has_prev:
                todo.append(("y_back", None))
            if n in (2, 6):
                ch = (n - 2) // 4
                if i < 2:
                    todo.append(("q", (0, i + 2, ch)))
                elif has_next:
                    todo.append(("q", (1, i - 2, ch)))
            if i == 1 and has_next:
                if n == 9:
                    todo.append(("x_turn", None))
                if n == 12:
                    todo.append(("k", None))
                if n == 14:
                    todo.append(("v", None))
            if i < QUADS - 1 or has_next:
                first, last = (n * 3 + 1) // 2, ((n + 1) * 3 + 1) // 2
                if n >= 8:
                    first, last = n + 4, n + 5
                for k in range(first, min(last, STEPS)):
                    todo.append(("max", k))
                if n == 13:
                    todo.append(("max_row", None))
            return todo

        def bodies(engine, body):
            body(0, False, True)
            with engine.Fori(1, B - 1) as b:
                body(b, True, True)
            body(B - 1, True, False)

        @block.sync
        def _(sp):
            def load_x(b):
                sp.dma_start(xs[:, TPB * b:TPB * (b + 1), :], x[b].rearrange("(j p) d -> p j d", p=P)).then_inc(s_x[b], 16)

            load_x(0)
            for r, a in ((R_B1, b1), (R_B2, b2), (R_B3, b3), (R_BQ, bq.rearrange("(c p) -> c p", p=P)),
                         (R_BO, bo.rearrange("(c p) -> c p", p=P))):
                sp.dma_start(brow[r:r + a.shape[0], :], a).then_inc(s_rows, 16)
            for c in range(2):
                sp.dma_start(brow[R_BK:R_BK + 1, DK * c:DK * (c + 1)], bk.rearrange("(c p) -> c p", p=DK)).then_inc(s_rows, 16)
            for b in range(1, B):
                load_x(b)
            sp.wait_ge(s_zero, 1)
            sp.dma_start(gws[:, 0:E], gate_w).then_inc(s_gb, 16)
            for j in range(TPB):
                sp.dma_start(gbc[SLOT * j:SLOT * j + E, :], gate_b.rearrange("(e c) -> e c", c=1)).then_inc(s_gb, 16)
            for t, a in ((w1s, w1), (w2s, w2), (w3s, w3)):
                sp.dma_start(t[:, :, :], a.rearrange("e d o -> d e o")).then_inc(s_wf, 16)
            sp.dma_start(wqs[:, :], Wq).then_inc(s_wa, 16)
            for c in range(2):
                sp.dma_start(wks[:, DK * c:DK * (c + 1)], Wk).then_inc(s_wa, 16)
            sp.dma_start(wvs[:, :], Wv).then_inc(s_wa, 16)
            sp.dma_start(wos[:, :, :], Wo.rearrange("(c p) n -> p c n", p=P)).then_inc(s_wa, 16)
            sp.dma_start(bvb[:, :], bv.partition_broadcast(P)).then_inc(s_wa, 16)

            def weights_out(f):
                s = F[f]
                sp.wait_ge(s["wT_ready"], 2)
                for j in range(TPB):
                    sp.dma_start(wd[:, :, j, :], wT[SLOT * j:SLOT * j + E, :, :]).then_inc(s["wd_written"], 16)
                sp.wait_ge(s["wd_written"], 16 * TPB)

                def load_wb(b, slot):
                    sp.dma_start(wb[:, slot, :, :], wd[:, b, :, :].rearrange("e j p -> e (j p)").partition_broadcast(P)
                                 ).then_inc(s["wb_loaded"], 16)

                load_wb(0, 0)
                sp.wait_ge(s["wb_loaded"], 16)
                load_wb(1, 1)
                with sp.Fori(1, B // 2) as c:
                    for slot in range(2):
                        sp.wait_ge(s["l3_bank_free"], 2 + E * (2 * c + slot - 1) + 1)
                        sp.dma_start(wb[:, slot, :, :], wd[:, bass.ds(2 * c + slot, 1), :, :].rearrange("e o j p -> e (o j p)")
                                     .partition_broadcast(P)).then_inc(s["wb_loaded"], 16)

            def place_max_row(b, i):
                wait(sp, s_x1d, x1_of_mt(b, i) + 1)
                sp.dma_start(QB[DK:DK + 1, i, :, :].rearrange("o h (j s) -> o (h j) s", j=TPB).bitcast(F32), mT[:, :].bitcast(F32)).then_inc(s_mrow, 16)

            def attention():
                place_max_row(0, 0)

                def body(b, has_prev, has_next):
                    for i in range(1, QUADS):
                        place_max_row(b, i)
                    if has_next:
                        place_max_row(b + 1, 0)

                bodies(sp, body)

            weights_out(0)
            attention()
            weights_out(1)
            for b in range(B):
                sp.wait_ge(F[1]["x_updated"], b + 1)
                sp.dma_start(out[b].rearrange("(j p) d -> p j d", p=P), xs[:, TPB * b:TPB * (b + 1), :]).then_inc(s_out, 16)
            sp.wait_ge(s_out, 16 * B)

        @block.gpsimd
        def _(pool):
            pool.memset(ident[:, :], 0.0).then_inc(s_id0, 1)
            pool.wait_ge(s_id0, 1)
            pool.affine_select(out=ident[:, :], in_=ident[:, :], compare_op=ALU.not_equal, fill=1.0, base=0,
                               pattern=[[-1, P]], channel_multiplier=1).then_inc(s_id, 1)

            def q_copy(b, i, ch):
                wait(pool, s_qhi, 2 * (QUADS * b + i) + ch + 1)
                q = QA[0:DK, i, 2 * ch:2 * ch + 2, :].bitcast(F32)
                one = ones[0:DK, 0:1].unsqueeze(2).to_broadcast([DK, 2, S])
                pool.tensor_tensor(QB[0:DK, i, 2 * ch:2 * ch + 2, :], q, one, ALU.mult).then_inc(s_qdup, 1)

            for i in range(2):
                for ch in range(2):
                    q_copy(0, i, ch)

            def body(b, has_prev, has_next):
                for i in range(QUADS):
                    for n in range(STEPS):
                        for stage, arg in side_steps(i, n, has_prev, has_next):
                            if stage == "q":
                                q_copy(b + arg[0], arg[1], arg[2])

            bodies(pool, body)

        @block.tensor
        def _(pe):
            pe.wait_ge(s_id, 1)
            pe.wait_ge(s_rows, 16 * 7)
            pe.transpose(psX[0][:, 0:ROWS], brow[:, :], ident[0:ROWS, 0:ROWS]).then_inc(s_bt, 1)

            def gate(f):
                s = F[f]

                def turn_x(b):
                    pe.wait_ge(s["xn_done"], TPB * (b + 1))
                    wait(pe, s["xnT_ready"], b - 1)
                    for j in range(TPB):
                        mm = pe.transpose(psX[b % 2][:, P * j:P * (j + 1)], xn[:, b % 2, j, :], ident[:, :])
                    mm.then_inc(s["xn_transposed"], 1)

                def logits(b):
                    pe.wait_ge(s["xnT_ready"], b + 1)
                    q = b % TPB
                    pe.matmul(psO[b // TPB][SLOT * q:SLOT * (q + 1), :], gws[:, :], xnT[:, b, :], start=True, stop=True
                              ).then_inc(s["logits_done"], 1)

                if f == 0:
                    pe.wait_ge(s_bc, 1)
                    pe.wait_ge(s_gb, 16 * (1 + TPB))
                else:
                    pe.wait_ge(s_x1d, X1_ALL)
                for b in range(B):
                    turn_x(b)
                    if b:
                        logits(b - 1)
                logits(B - 1)
                for g in range(GROUPS):
                    pe.wait_ge(s["probs_ready"], g + 1)
                    if g == 0:
                        pe.wait_ge(s["xnT_ready"], B)
                    for j in range(TPB):
                        mm = pe.transpose(psX[g][:, P * j:P * (j + 1)], prs[:, g, P * j:P * (j + 1)], ident[:, :])
                    mm.then_inc(s["probs_transposed"], 1)
                pe.wait_ge(s["picked"], 1)
                for src, banks in ((indp, psS), (wp, psP)):
                    for b in range(B):
                        q = b % TPB
                        mm = pe.transpose(banks[b // TPB][:, P * q:P * (q + 1)],
                                          src[:, TPB * b:TPB * (b + 1), :].rearrange("p t e -> p (t e)"), ident[:, :])
                        if q == TPB - 1:
                            mm.then_inc(s["picks_transposed"], 1)
                pe.matmul(psX[0][:, 0:NT * E], ones[:, :], wtok[:, :, :].rearrange("p t e -> p (t e)"), start=True, stop=True
                          ).then_inc(s["picks_transposed"], 1)

            def experts(f):
                s = F[f]

                def layer1(e, m, rhs):
                    wait(pe, s["relu1_done"], m - 1)
                    pe.matmul(psS[e % 2][:, :], w1s[:, e, :], rhs, start=True, stop=True).then_inc(s["l1_done"], 1)

                def layer2(e, m):
                    pe.wait_ge(s["relu1_done"], m + 1)
                    wait(pe, s["relu2_done"], m - 1)
                    pe.matmul(psP[e % 2][:, :], w2s[:, e, :], h1[:, e % 2, :], start=True, stop=True).then_inc(s["l2_done"], 1)

                def layer3(e, m):
                    pe.wait_ge(s["relu2_done"], m + 1)
                    pe.wait_ge(s["l3_bank_free"], m + 1)
                    pe.matmul(psO[e % 2][:, :], w3s[:, e, :], h2[:, e % 2, :], start=True, stop=True).then_inc(s["l3_done"], 1)

                if f == 0:
                    pe.wait_ge(s_wf, 48)
                pe.wait_ge(s["indT_ready"], GROUPS)
                pe.wait_ge(s["wT_ready"], GROUPS)
                layer1(0, 0, xnT[:, 0, :])
                layer1(1, 1, xnT[:, 0, :])
                layer2(0, 0)

                def body(b, has_next):
                    for e in range(E):
                        m = E * b + e
                        if e + 2 < E:
                            layer1(e + 2, m + 2, xnT[:, at(b), :].rearrange("p o s -> p (o s)"))
                        elif has_next:
                            layer1(e + 2 - E, m + 2, xnT[:, at(b + 1), :].rearrange("p o s -> p (o s)"))
                        if e + 1 < E:
                            layer2(e + 1, m + 1)
                        elif has_next:
                            layer2(0, m + 1)
                        layer3(e, m)

                body(0, True)
                with pe.Fori(1, B - 1) as b:
                    body(b, True)
                body(B - 1, False)

            def update(f):
                s = F[f]
                pe.wait_ge(s["v_ready"], 1)
                pe.wait_ge(s["wsum_done"], 1)
                pe.transpose(psX[0][:, 0:P], vrep[:, :, :].rearrange("p j e -> p (j e)"), ident[:, :]).then_inc(s["v_transposed"], 1)
                pe.wait_ge(s["VB_ready"], 1)
                for b in range(B):
                    wait(pe, s["x_updated"], b - 1)
                    pe.matmul(psS[b % 2][:, :], indT[:, b, :], VB[:, :, :].rearrange("p j d -> p (j d)"), start=True, stop=True
                              ).then_inc(s["update_done"], 1)

            def x_turn(b):
                pe.wait_ge(s_axn, b + 1)
                wait(pe, s_x1d, x1_of_xt(b))
                for j in range(TPB):
                    mm = pe.transpose(X1[:, P * j:P * (j + 1)], xn[:, 0, j, :], ident[:, :])
                mm.then_inc(s_x1f, 1)

            def k_proj(b):
                wait(pe, s_x1d, x1_of_xt(b) + 1)
                wait(pe, s_x0d, x0_of_k(b))
                pe.matmul(X0[:, :], wks[:, :], xaT, start=True, stop=True).then_inc(s_x0f, 1)

            def v_proj(b):
                wait(pe, s_x0d, x0_of_v(b))
                for j in range(TPB):
                    mm = pe.matmul(X0[:, DK * j:DK * (j + 1)], xaT[:, P * j:P * (j + 1)], wvs[:, :], start=True, stop=True)
                mm.then_inc(s_x0f, 1)

            def q_proj(b, i, ch):
                c = 2 * i + ch
                wait(pe, s_x0d, x0_of_q(b, i, ch))
                pe.matmul(X0[:, :], wqs[:, P * c:P * (c + 1)], xaT, start=True, stop=True).then_inc(s_x0f, 1)

            def scores_for_max(b, i, k):
                g = QUADS * b + i
                if k == 0:
                    wait(pe, s_x0d, x0_of_q(b, i, 1) + 1)
                    if i == 0:
                        pe.wait_ge(s_khi, b + 1)
                wait(pe, s_max, STEPS * g + k - 1)
                h, j = k // TPB, k % TPB
                pe.matmul(psS[k % 2][:, :], QA[:, i, h, P * j:P * (j + 1)], (KAn if i == 0 else KA)[:, :], start=True, stop=True
                          ).then_inc(s_s, 1)

            def turn_max(b, i):
                pe.wait_ge(s_max, STEPS * (QUADS * b + i + 1))
                wait(pe, s_x1d, x1_of_mt(b, i))
                pe.transpose(X1[0:STEPS, 0:P], mx[:, i % 2, :], ident[:, :]).then_inc(s_x1f, 1)

            def scores(b, i, n):
                g = QUADS * b + i
                N = STEPS * g + n
                h, t = n // TPB, n % TPB
                if n == 0:
                    pe.wait_ge(s_mrow, 16 * (g + 1))
                    pe.wait_ge(s_qdup, 2 * (g + 1))
                    if i == 0:
                        pe.wait_ge(s_sw, b + 1)
                wait(pe, s_exp, N - 1)
                ps = psP[n % 2][:, :]
                pe.matmul(ps, KA[:, P * t:P * (t + 1)], QA[:, i, h, :], start=True, stop=False)
                pe.matmul(ps, KB[:, P * t:P * (t + 1)], QB[:, i, h, :], start=False, stop=True).then_inc(s_st, 1)

            def weigh(b, i, n):
                N = STEPS * (QUADS * b + i) + n
                h, t = n // TPB, n % TPB
                if t == 0:
                    wait(pe, s_on, HPQ * (QUADS * b + i) + h - 1)
                pe.wait_ge(s_exp, N + 1)
                pe.matmul(psO[h % 2][:, :], V[:, t, :], PT[:, n % 4, :], start=(t == 0), stop=(t == TPB - 1)).then_inc(s_pv, 1)

            def out_proj(b):
                wait(pe, s_x1d, x1_of_op(b))
                pe.wait_ge(s_on, H * (b + 1))
                for c in range(NCH):
                    mm = pe.matmul(X1[:, :], wos[:, c, :], OT[:, c, :], start=(c == 0), stop=(c == NCH - 1))
                mm.then_inc(s_x1f, 1)

            def y_back(b):
                wait(pe, s_x1d, x1_of_yt(b))
                for j in range(TPB):
                    mm = pe.transpose(X1[:, P * j:P * (j + 1)], yT[:, P * j:P * (j + 1)], ident[:, :])
                mm.then_inc(s_x1f, 1)

            def attention():
                pe.wait_ge(F[0]["x_updated"], B)
                pe.wait_ge(s_wa, 16 * 6)
                x_turn(0)
                k_proj(0)
                v_proj(0)
                for i in range(2):
                    for ch in range(2):
                        q_proj(0, i, ch)
                for k in range(STEPS):
                    scores_for_max(0, 0, k)
                turn_max(0, 0)

                def body(b, has_prev, has_next):
                    for i in range(QUADS):
                        for n in range(STEPS):
                            scores(b, i, n)
                            for stage, arg in side_steps(i, n, has_prev, has_next):
                                nb, ni = (b, i + 1) if i + 1 < QUADS else (b + 1, 0)
                                if stage == "y_back":
                                    y_back(b - 1)
                                elif stage == "q":
                                    q_proj(b + arg[0], arg[1], arg[2])
                                elif stage == "x_turn":
                                    x_turn(b + 1)
                                elif stage == "k":
                                    k_proj(b + 1)
                                elif stage == "v":
                                    v_proj(b + 1)
                                elif stage == "max":
                                    scores_for_max(nb, ni, arg)
                                elif stage == "max_row":
                                    turn_max(nb, ni)
                            if n:
                                weigh(b, i, n - 1)
                            elif i:
                                weigh(b, i - 1, STEPS - 1)
                    weigh(b, QUADS - 1, STEPS - 1)
                    out_proj(b)

                bodies(pe, body)
                y_back(B - 1)

            gate(0)
            experts(0)
            update(0)
            attention()
            gate(1)
            experts(1)
            update(1)

        @block.scalar
        def _(act):
            act.wait_ge(s_bt, 1)
            act.copy(bcol[:, :], psX[0][:, 0:ROWS]).then_inc(s_bc, 1)

            def root(k):
                act.wait_ge(s_var, k + 1)
                act.activation(std[:, :], var[:, :], ACT.Sqrt).then_inc(s_std, 1)

            def gate(f):
                s = F[f]
                for b in range(B):
                    act.wait_ge(s["xn_transposed"], b + 1)
                    act.copy(xnT[:, b, :], psX[b % 2][:, :]).then_inc(s["xnT_ready"], 1)
                for g in range(GROUPS):
                    act.wait_ge(s["logits_biased"], g + 1)
                    act.activation(prs[:, g, :], lgs[:, :], ACT.Exp, bias=gst[:, g, 0:1], accum_out=gst[:, g, 1:2]
                                   ).then_inc(s["gate_exp"], 1)
                for g in range(GROUPS):
                    act.wait_ge(s["picks_transposed"], GROUPS + g + 1)
                    act.copy(wT[:, TPB * g:TPB * (g + 1), :].rearrange("p b t -> p (b t)"), psP[g][:, :]).then_inc(s["wT_ready"], 1)

            def experts(f):
                s = F[f]

                def relu1(e, m):
                    act.wait_ge(s["l1_done"], m + 1)
                    wait(act, s["l2_done"], m - 1)
                    act.activation(h1[:, e % 2, :], psS[e % 2][:, :], ACT.Relu, bias=bcol[:, R_B1 + e:R_B1 + e + 1]
                                   ).then_inc(s["relu1_done"], 1)

                def relu2(e, m):
                    act.wait_ge(s["l2_done"], m + 1)
                    wait(act, s["l3_done"], m - 1)
                    act.activation(h2[:, e % 2, :], psP[e % 2][:, :], ACT.Relu, bias=bcol[:, R_B2 + e:R_B2 + e + 1]
                                   ).then_inc(s["relu2_done"], 1)

                relu1(0, 0)
                relu1(1, 1)
                relu2(0, 0)

                def body(b, has_next):
                    for e in range(E):
                        m = E * b + e
                        if e + 2 < E or has_next:
                            relu1((e + 2) % E, m + 2)
                        if e + 1 < E or has_next:
                            relu2((e + 1) % E, m + 1)

                body(0, True)
                with act.Fori(1, B - 1) as b:
                    body(b, True)
                body(B - 1, False)

            def x_turned(b):
                wait(act, s_x1f, x1_of_xt(b) + 1)
                if not (isinstance(b, int) and b == 0):
                    act.wait_ge(s_x0f, x0_of_q(b - 1, QUADS - 1, 1) + 1)
                act.copy(xaT, X1[:, :]).then_inc(s_x1d, 1)

            def k_high(b):
                wait(act, s_x0f, x0_of_k(b) + 1)
                wait(act, s_sw, b)
                if not (isinstance(b, int) and b == 0):
                    act.wait_ge(s_s, STEPS * (QUADS * (b - 1) + 1))
                act.activation(KAn[:, :], X0[:, :], ACT.Identity, bias=bcol[:, R_BK:R_BK + 1]).then_inc(s_khi, 1)

            def q_high(b, i, ch):
                c = 2 * i + ch
                wait(act, s_x0f, x0_of_q(b, i, ch) + 1)
                wait(act, s_st, STEPS * (QUADS * b + i - QUADS + 1))
                for r in range(2):
                    ins = act.activation(QA[0:DK, i, 2 * ch + r, :], X0[DK * r:DK * (r + 1), :], ACT.Identity,
                                         bias=bcol[DK * r:DK * (r + 1), R_BQ + c:R_BQ + c + 1])
                ins.then_inc(s_qhi, 1)

            def exponent(b, i, n):
                N = STEPS * (QUADS * b + i) + n
                act.wait_ge(s_st, N + 1)
                wait(act, s_pv, N - 3)
                act.activation(PT[:, n % 4, :], psP[n % 2][:, :], ACT.Exp, scale=SCALE).then_inc(s_exp, 1)

            def y_bias(b):
                wait(act, s_x1f, x1_of_op(b) + 1)
                act.activation(yT, X1[:, :], ACT.Identity, bias=bcol[:, R_BO:R_BO + 1]).then_inc(s_x1d, 1)

            def attention():
                x_turned(0)
                k_high(0)
                for i in range(2):
                    for ch in range(2):
                        q_high(0, i, ch)

                def body(b, has_prev, has_next):
                    for i in range(QUADS):
                        for n in range(STEPS):
                            exponent(b, i, n)
                            for stage, arg in side_steps(i, n, has_prev, has_next):
                                if stage == "q":
                                    q_high(b + arg[0], arg[1], arg[2])
                                elif stage == "x_turn":
                                    x_turned(b + 1)
                                elif stage == "k":
                                    k_high(b + 1)
                    y_bias(b)

                bodies(act, body)

            root(0)
            gate(0)
            experts(0)
            root(1)
            attention()
            root(2)
            gate(1)
            experts(1)

        @block.vector
        def _(dve):
            for t in (gws, gbc, indp, wp, vrep, VB):
                dve.memset(t[tuple(slice(None) for _ in t.shape)], 0.0)
            dve.memset(ones[:, :], 1.0)
            for e in range(E):
                dve.memset(prio[:, e:e + 1], float(E - e))
            dve.memset(V[:, :, DK:2 * DK], 1.0)
            dve.memset(lgs[0:1, :], -1.0).then_inc(s_rz, 1)
            dve.wait_ge(s_rz, 1)
            dve.tensor_copy(KB[DK:DK + 1, :], lgs[0:1, :]).then_inc(s_zero, 1)

            ln_count = [0]

            def ln_link(ins):
                ln_count[0] += 1
                ins.then_inc(s_ln, 1)
                dve.wait_ge(s_ln, ln_count[0])

            def token_stats(k):
                for t in range(NT):
                    if k == 0 and t % TPB == 0:
                        dve.wait_ge(s_x[t // TPB], 16)
                    ins = dve.bn_stats(stats[:, t, :], xs[:, t, :])
                ins.then_inc(s_stats, 1)
                dve.wait_ge(s_stats, k + 1)
                ln_link(dve.tensor_tensor(mean[:, :], stats[:, :, 1], stats[:, :, 4], ALU.add))
                ln_link(dve.tensor_tensor(mdif[:, :], stats[:, :, 1], stats[:, :, 4], ALU.subtract))
                ln_link(dve.tensor_tensor(var[:, :], stats[:, :, 2], stats[:, :, 5], ALU.add))
                ln_link(dve.tensor_tensor(sq[:, :], mdif[:, :], mdif[:, :], ALU.mult))
                ln_link(dve.tensor_scalar(var[:, :], var[:, :], 1.0 / D, EPS, ALU.mult, ALU.add))
                ln_link(dve.tensor_scalar(mean[:, :], mean[:, :], 0.5, None, ALU.mult))
                dve.scalar_tensor_tensor(out=var[:, :], in0=sq[:, :], scalar=0.25, in1=var[:, :], op0=ALU.mult, op1=ALU.add
                                         ).then_inc(s_var, 1)
                dve.wait_ge(s_std, k + 1)
                ln_link(dve.reciprocal(rstd[:, :], std[:, :]))

            def gate(f):
                s = F[f]
                for b in range(B):
                    wait(dve, s["xn_transposed"], b - 1)
                    for j in range(TPB):
                        t = TPB * b + j
                        dve.tensor_scalar(xn[:, b % 2, j, :], xs[:, t, :], mean[:, t:t + 1], rstd[:, t:t + 1],
                                          ALU.subtract, ALU.mult).then_inc(s["xn_done"], 1)
                count = [0]

                def link(ins):
                    count[0] += 1
                    ins.then_inc(s["gate_chain"], 1)
                    dve.wait_ge(s["gate_chain"], count[0])

                if f == 0:
                    dve.wait_ge(s_gb, 16 * (1 + TPB))
                for g in range(GROUPS):
                    dve.wait_ge(s["logits_done"], TPB * (g + 1))
                    wait(dve, s["gate_exp"], g)
                    link(dve.tensor_scalar(lgs[:, :], psO[g][:, :], gbc[:, 0:1], None, ALU.add))
                    dve.tensor_reduce(gst[:, g, 0:1], lgs[:, :], AX.X, ALU.max, negate=True).then_inc(s["logits_biased"], 1)
                    dve.wait_ge(s["gate_exp"], g + 1)
                    link(dve.reciprocal(gst[:, g, 2:3], gst[:, g, 1:2]))
                    dve.tensor_scalar(prs[:, g, :], prs[:, g, :], gst[:, g, 2:3], None, ALU.mult).then_inc(s["probs_ready"], 1)
                for g in range(GROUPS):
                    dve.wait_ge(s["probs_transposed"], g + 1)
                    src = psX[g][:, :].rearrange("p (j b e) -> p b j e", j=TPB, b=TPB)[:, :, :, 0:E]
                    dst = pt[:, TPB * TPB * g:TPB * TPB * (g + 1), :].rearrange("p (b j) e -> p b j e", b=TPB)
                    for q in range(TPB):
                        ins = dve.tensor_copy(dst[:, q], src[:, q])
                    link(ins)
                tmb = tm[:, :].unsqueeze(2).to_broadcast([P, NT, E])
                prb = prio[:, :].unsqueeze(1).to_broadcast([P, NT, E])
                for oh, left in ((oh1, pt), (oh2, tb)):
                    link(dve.tensor_reduce(tm[:, :], left[:, :, :], AX.X, ALU.max))
                    link(dve.tensor_tensor(ta[:, :, :], left[:, :, :], tmb, ALU.is_equal))
                    link(dve.tensor_tensor(ta[:, :, :], ta[:, :, :], prb, ALU.mult))
                    link(dve.tensor_reduce(tm[:, :], ta[:, :, :], AX.X, ALU.max))
                    link(dve.tensor_tensor(oh[:, :, :], ta[:, :, :], tmb, ALU.is_equal))
                    if oh is oh1:
                        link(dve.scalar_tensor_tensor(out=tb[:, :, :], in0=oh[:, :, :], scalar=-2.0, in1=pt[:, :, :],
                                                      op0=ALU.mult, op1=ALU.add))
                link(dve.tensor_tensor(indp[:, :, 0:E], oh1[:, :, :], oh2[:, :, :], ALU.add))
                link(dve.tensor_tensor(wtok[:, :, :], indp[:, :, 0:E], pt[:, :, :], ALU.mult))
                dve.tensor_copy(wp[:, :, 0:E], wtok[:, :, :]).then_inc(s["picked"], 1)
                for g in range(GROUPS):
                    dve.wait_ge(s["picks_transposed"], g + 1)
                    dve.tensor_copy(indT[:, TPB * g:TPB * (g + 1), :].rearrange("p b t -> p (b t)"), psS[g][:, :]
                                    ).then_inc(s["indT_ready"], 1)
                dve.wait_ge(s["picks_transposed"], 2 * GROUPS + 1)
                dve.tensor_reduce(wsum[:, :], psX[0][:, 0:NT * E].rearrange("p (t e) -> p e t", e=E), AX.X, ALU.add
                                  ).then_inc(s["wsum_done"], 1)

            def experts(f):
                s = F[f]
                dve.tensor_scalar(nb3[:, :], bcol[:, R_B3:R_B3 + E], -1.0, None, ALU.mult).then_inc(s["l3_bank_free"], 2)
                dve.wait_ge(s["l3_bank_free"], 2)

                def body(c, slot):
                    b = 2 * c + slot
                    dve.wait_ge(s["wb_loaded"], 16 * b + 16)
                    for e in range(E):
                        dve.wait_ge(s["l3_done"], E * b + e + 1)
                        z = psO[e % 2][:, :]
                        dve.scalar_tensor_tensor(out=z, in0=z, scalar=nb3[:, e:e + 1], in1=wb[:, slot, e, :], op0=ALU.max,
                                                 op1=ALU.mult, accum_out=vacc[:, e, bass.ds(b, 1)]
                                                 ).then_inc(s["l3_bank_free"], 1)

                with dve.Fori(0, B // 2) as c:
                    for slot in range(2):
                        body(c, slot)

            def update(f):
                s = F[f]
                count = [0]

                def link(ins):
                    count[0] += 1
                    ins.then_inc(s["v_chain"], 1)
                    dve.wait_ge(s["v_chain"], count[0])

                dve.wait_ge(s["l3_bank_free"], 2 + B * E)
                dve.wait_ge(s["wsum_done"], 1)
                link(dve.tensor_reduce(vv[:, 0, :], vacc[:, :, :], AX.X, ALU.add))
                link(dve.tensor_tensor(vv[:, 1, :], bcol[:, R_B3:R_B3 + E], wsum[:, :], ALU.mult))
                link(dve.tensor_tensor(vv[:, 0, :], vv[:, 0, :], vv[:, 1, :], ALU.add))
                dve.tensor_scalar(vrep[:, :, 0:E], vv[:, 0:1, :].to_broadcast([P, TPB, E]), 0.5, None, ALU.mult
                                  ).then_inc(s["v_ready"], 1)
                dve.wait_ge(s["v_transposed"], 1)
                for j in range(TPB):
                    ins = dve.tensor_copy(VB[SLOT * j:SLOT * (j + 1), j, :], psX[0][SLOT * j:SLOT * (j + 1), 0:P])
                ins.then_inc(s["VB_ready"], 1)
                for b in range(B):
                    dve.wait_ge(s["update_done"], b + 1)
                    xb = xs[:, TPB * b:TPB * (b + 1), :].rearrange("p j d -> p (j d)")
                    dve.tensor_tensor(xb, xb, psS[b % 2][:, :], ALU.add).then_inc(s["x_updated"], 1)

            def x_normal(b):
                wait(dve, s_x1f, 0 if isinstance(b, int) and b == 0 else x1_of_xt(b - 1) + 1)
                for j in range(TPB):
                    t = at(TPB * b + j)
                    ins = dve.tensor_scalar(xn[:, 0, j, :], xs[:, t, :].rearrange("p o d -> p (o d)"), mean[:, t], rstd[:, t],
                                            ALU.subtract, ALU.mult)
                ins.then_inc(s_axn, 1)

            def k_low(b):
                dve.wait_ge(s_khi, b + 1)
                dve.scalar_tensor_tensor(out=KBn[:, :], in0=X0[0:DK, :], scalar=bcol[0:DK, R_BK:R_BK + 1], in1=KAn[0:DK, :],
                                         op0=ALU.add, op1=ALU.subtract).then_inc(s_x0d, 1)

            def v_bias(b):
                wait(dve, s_x0f, x0_of_v(b) + 1)
                dve.tensor_tensor(Vn[:, :, :], X0[:, 0:TPB * DK].rearrange("p (j d) -> p j d", j=TPB),
                                  bvb[:, :].unsqueeze(1).to_broadcast([P, TPB, DK]), ALU.add).then_inc(s_x0d, 1)

            def q_low(b, i, ch):
                c = 2 * i + ch
                wait(dve, s_qhi, 2 * (QUADS * b + i) + ch + 1)
                for r in range(2):
                    rows = slice(DK * r, DK * (r + 1))
                    ins = dve.scalar_tensor_tensor(out=QA[DK:2 * DK, i, 2 * ch + r, :], in0=X0[rows, :],
                                                   scalar=bcol[rows, R_BQ + c:R_BQ + c + 1], in1=QA[0:DK, i, 2 * ch + r, :],
                                                   op0=ALU.add, op1=ALU.subtract)
                ins.then_inc(s_x0d, 1)

            def row_max(b, i, k):
                dve.wait_ge(s_s, STEPS * (QUADS * b + i) + k + 1)
                dve.tensor_reduce(mx[:, i % 2, k:k + 1], psS[k % 2][:, :], AX.X, ALU.max).then_inc(s_max, 1)

            def max_turned(b, i):
                wait(dve, s_x1f, x1_of_mt(b, i) + 1)
                wait(dve, s_mrow, 16 * (QUADS * b + i))
                dve.tensor_copy(mT[:, :], X1[0:STEPS, 0:P]).then_inc(s_x1d, 1)

            def switch(b):
                wait(dve, s_pv, H * TPB * b)
                wait(dve, s_x0d, x0_of_v(b) + 1)
                dve.tensor_copy(KA[:, :], KAn[:, :])
                dve.tensor_copy(KB[0:DK, :], KBn[:, :])
                dve.tensor_copy(V[:, :, 0:DK], Vn[:, :, :]).then_inc(s_sw, 1)

            def normalise(b, i, h):
                hd = H * b + HPQ * i + h
                dve.wait_ge(s_pv, TPB * (hd + 1))
                wait(dve, s_on, hd)
                dve.reciprocal(rz, psO[h % 2][DK:2 * DK, :]).then_inc(s_rz, 1)
                if not (isinstance(b, int) and b == 0):
                    dve.wait_ge(s_x1f, x1_of_op(b - 1) + 1)
                dve.wait_ge(s_rz, hd + 2)
                dve.tensor_tensor(OT[DK * (h % 2):DK * (h % 2 + 1), 2 * i + h // 2, :], psO[h % 2][0:DK, :], rz, ALU.mult
                                  ).then_inc(s_on, 1)

            def add_y(b):
                wait(dve, s_x1f, x1_of_yt(b) + 1)
                xb = xs[:, at(TPB * b, TPB), :]
                dve.tensor_tensor(xb, xb, X1[:, :].rearrange("p (j d) -> p j d", j=TPB), ALU.add).then_inc(s_x1d, 1)

            def attention():
                x_normal(0)
                k_low(0)
                v_bias(0)
                switch(0)
                for i in range(2):
                    for ch in range(2):
                        q_low(0, i, ch)
                for k in range(STEPS):
                    row_max(0, 0, k)
                max_turned(0, 0)

                def body(b, has_prev, has_next):
                    for i in range(QUADS):
                        for n in range(STEPS):
                            if i == 1 and n == 7 and has_next:
                                x_normal(b + 1)
                            for stage, arg in side_steps(i, n, has_prev, has_next):
                                nb, ni = (b, i + 1) if i + 1 < QUADS else (b + 1, 0)
                                if stage == "y_back":
                                    add_y(b - 1)
                                elif stage == "q":
                                    q_low(b + arg[0], arg[1], arg[2])
                                elif stage == "k":
                                    k_low(b + 1)
                                elif stage == "v":
                                    v_bias(b + 1)
                                elif stage == "max":
                                    row_max(nb, ni, arg)
                                elif stage == "max_row":
                                    max_turned(nb, ni)
                            if n and n % TPB == 0:
                                normalise(b, i, n // TPB - 1)
                            elif n == 0 and i:
                                normalise(b, i - 1, HPQ - 1)
                    normalise(b, QUADS - 1, HPQ - 1)
                    if has_next:
                        switch(b + 1)

                bodies(dve, body)
                add_y(B - 1)

            token_stats(0)
            dve.wait_ge(s_bc, 1)
            gate(0)
            experts(0)
            update(0)
            dve.wait_ge(F[0]["x_updated"], B)
            token_stats(1)
            attention()
            dve.wait_ge(s_x1d, X1_ALL)
            token_stats(2)
            gate(1)
            experts(1)
            update(1)


_INS = ["L0_attn_x", "L0_attn_Wq", "L0_attn_bq", "L0_attn_Wk", "L0_attn_bk", "L0_attn_Wv", "L0_attn_bv", "L0_attn_Wo",
        "L0_attn_bo", "L0_ffn_gate_w", "L0_ffn_gate_b", "L0_ffn_w1", "L0_ffn_b1", "L0_ffn_w2", "L0_ffn_b2", "L0_ffn_w3",
        "L0_ffn_b3"]


def kernel(**inputs):
    import numpy as _np
    import concourse.bacc as _bacc
    from concourse import mybir as _mybir
    from concourse.bass_utils import run_bass_kernel_spmd as _run

    nc = _bacc.Bacc("TRN2", target_bir_lowering=False, num_devices=1)
    arrays, args = {}, []
    for name in _INS:
        a = _np.ascontiguousarray(inputs[name])
        arrays[f"in_{name}"] = a
        args.append(nc.dram_tensor(f"in_{name}", a.shape, _mybir.dt.from_np(a.dtype), kind="ExternalInput").ap())
    shape = inputs["L0_attn_x"].shape
    args.append(nc.dram_tensor("out_0", shape, _mybir.dt.float32, kind="ExternalOutput").ap())
    macaron_kernel(nc, *args)
    r = _run(nc, [arrays], core_ids=[0])
    return r.results[0]["out_0"]
```

```python
from contextlib import ExitStack

import concourse.bass as bass
from concourse import mybir

F32 = mybir.dt.float32
F32R = mybir.dt.float32r
ALU = mybir.AluOpType
ACT = mybir.ActivationFunctionType
AX = mybir.AxisListType

P = 128
EPS = 1e-5


def wait(engine, semaphore, value):
    if isinstance(value, int) and value <= 0:
        return
    engine.wait_ge(semaphore, value)


def at(start, count=1):
    return slice(start, start + count) if isinstance(start, int) else bass.ds(start, count)


def macaron_kernel(nc, x, Wq, bq, Wk, bk, Wv, bv, Wo, bo, gate_w, gate_b, w1, b1, w2, b2, w3, b3, out):
    B, S, D = x.shape
    E = gate_w.shape[1]
    DK = Wk.shape[1]
    H = Wq.shape[1] // DK
    TPB = S // P
    NT = B * TPB
    NCH = H * DK // P
    SLOT = 32
    GROUPS = B // TPB
    QUADS = H // TPB
    HPQ = H // QUADS
    STEPS = HPQ * TPB
    SCALE = float(DK) ** -0.5
    assert D == P and E == 8 and DK == 64 and TPB == 4 and HPQ == 4

    with ExitStack() as ctx:
        def sb(name, shape, dt=F32):
            return ctx.enter_context(nc.sbuf_tensor(name, shape, dt))

        def bank(name):
            return ctx.enter_context(nc.psum_tensor(name, [P, 512], F32))

        def sem(name):
            return ctx.enter_context(nc.semaphore(name))

        xs = sb("xs", [P, NT, D])
        ident = sb("ident", [P, P])
        ones = sb("ones", [P, P])
        whi = sb("whi", [P, 3, E, P], F32R)
        wlo = sb("wlo", [P, 3, E, P], F32R)
        wqhi = sb("wqhi", [P, H * DK], F32R)
        wqlo = sb("wqlo", [P, H * DK], F32R)
        gws = sb("gws", [P, SLOT])
        wks = sb("wks", [P, 2 * DK])
        wvs = sb("wvs", [P, DK])
        wos = sb("wos", [P, NCH, D])
        R_B1, R_B2, R_B3, R_BQ, R_BO, R_BK, ROWS = 0, E, 2 * E, 3 * E, 3 * E + NCH, 3 * E + NCH + 1, 3 * E + NCH + 2
        bcol = sb("bcol", [P, ROWS])
        nb3 = sb("nb3", [P, E])
        gbc = sb("gbc", [P, 1])
        bvb = sb("bvb", [P, DK])
        prio = sb("prio", [P, E])
        stats = sb("stats", [P, NT, 6])
        mean = sb("mean", [P, NT])
        mdif = sb("mdif", [P, NT])
        var = sb("var", [P, NT])
        sq = sb("sq", [P, NT])
        std = sb("std", [P, NT])
        rstd = sb("rstd", [P, NT])
        xn = sb("xn", [P, 2, TPB, D])
        xnT = sb("xnT", [P, B, S])
        wb0 = sb("wb_even", [P, E, S], F32R)
        wb1 = sb("wb_odd", [P, E, S])
        wbs = (wb0[:, :, :].bitcast(F32), wb1[:, :, :])
        gst = sb("gst", [P, GROUPS, 4])
        tm = sb("tm", [P, NT])
        indp = sb("indp", [P, NT, SLOT])
        picksT = sb("picksT", [P, 2, B, P])
        indT, wT = (picksT[:, u] for u in range(2))
        t1 = xn[:, :, :, :].rearrange("p u j d -> p u (j d)")
        t2 = sb("t2", [P, 2, S])
        wraw = [picksT[:, 0, :, :].rearrange("p b t -> p (b t)"), picksT[:, 1, :, :].rearrange("p b t -> p (b t)"),
                t2[:, :, :].rearrange("p u s -> p (u s)"), wos[:, :, :].rearrange("p c n -> p (c n)")]
        vacc = sb("vacc", [P, E, B])
        wsum = sb("wsum", [P, E])
        vv = sb("vv", [P, 2, E])
        vrep = sb("vrep", [P, TPB, SLOT])
        VB = xn[:, 0, :, :]
        wd = nc.dram_tensor("wd", [E, B, TPB, P], F32, kind="Internal").ap()
        prs = wb1[:, 0:GROUPS, :]
        lgs = wb1[:, 2, :]
        wp = wb1[:, 3:5, :].rearrange("p u s -> p (u s)").rearrange("p (t e) -> p t e", e=SLOT)

        def small(k):
            return wb1[:, 5 + k // 2, 256 * (k % 2):256 * (k % 2 + 1)].rearrange("p (t e) -> p t e", e=E)

        pt, ta, tb, oh1, oh2, wtok = (small(k) for k in range(6))
        brow = wb1[0:ROWS, 4, 0:P]
        QA = sb("QA", [P, QUADS, HPQ, S], F32R)
        QB = sb("QB", [P, QUADS, HPQ, S], F32R)
        XA = sb("XA", [P, 2, S], F32R)
        KA = sb("KA", [P, S], F32R)
        KB = sb("KB", [P, S], F32R)
        KAn = sb("KAn", [P, S], F32R)
        KBn_mT = sb("KBn_mT", [P, S], F32R)
        KBn = KBn_mT[0:DK, :]
        mT = KBn_mT[DK:DK + STEPS, 0:P]
        Vh = sb("Vh", [P, TPB, 3, DK], F32R)
        Vl = sb("Vl", [P, TPB, 3, DK], F32R)
        mx = sb("mx", [P, 2, STEPS])
        rzd = nc.dram_tensor("rzd", [2, 2, 2, S], F32, kind="Internal").ap()
        OT = xnT
        PT = picksT[:, :, :, :].rearrange("p u b t -> p (u b t)").rearrange("p (n s) -> p n s", s=S)
        PD = 4
        Ph, Pl = wb0[:, 0:PD, :], wb0[:, PD:2 * PD, :]
        xaT = t1[:, 1, :]
        yT = t2[:, 1, :]
        rzb = indp[:, :, :].rearrange("p t e -> p (t e)").rearrange("p (u s) -> p u s", s=S)
        Vn = t2[:, 0, 0:TPB * DK].rearrange("p (j d) -> p j d", j=TPB)
        zc = t2[0:HPQ * 16, 0, TPB * DK:TPB * DK + S // 16]
        rc = t2[0:HPQ * 16, 0, TPB * DK + S // 16:TPB * DK + 2 * S // 16]
        OZ = wb1
        xh = QB[:, 0:2, :, :].rearrange("p u h s -> p (u h) s")
        xl = QB[:, 2:4, :, :].rearrange("p u h s -> p (u h) s")
        h1h, h1l, h2h, h2l = (QA[:, k, 0:2, :] for k in range(4))

        psS = [bank("psS0"), bank("psS1")]
        psP = [bank("psP0"), bank("psP1")]
        psO = [bank("psO0"), bank("psO1")]
        X0, X1 = psX = [bank("psX0"), bank("psX1")]

        s_x = [sem(f"x_loaded{b}") for b in range(B)]
        s_wf = sem("split_weights_loaded")
        s_wh = sem("weights_high")
        s_wl = sem("weights_low")
        s_wa = sem("attn_weights_loaded")
        s_rows = sem("bias_rows_loaded")
        s_gb = sem("gate_bias_loaded")
        s_zero = sem("zeroed")
        s_id0 = sem("ident_zeroed")
        s_id = sem("ident_ready")
        s_bt = sem("bias_transposed")
        s_bc = sem("bias_columns")
        s_nb3 = sem("negated_b3")
        s_stats = sem("token_stats")
        s_ln = sem("ln_chain")
        s_var = sem("variance_ready")
        s_std = sem("std_ready")

        def ffn_sems(f):
            names = ("xn_done", "xn_transposed", "xnT_ready", "logits_done", "gate_chain", "logits_biased",
                     "gate_exp", "probs_ready", "probs_transposed", "picked", "picks_transposed", "indT_ready",
                     "wT_ready", "wsum_done", "wd_written", "wb_loaded", "l1_done", "l2_done", "l3_done",
                     "relu1_done", "relu2_done", "l3_bank_free", "h1_high", "h1_ready", "h2_high", "h2_ready",
                     "x_low", "pads_zeroed", "v_chain", "v_ready", "v_transposed",
                     "VB_ready", "update_done", "x_updated")
            return {n: sem(f"f{f}_{n}") for n in names}

        F = [ffn_sems(0), ffn_sems(1)]
        s_axn = sem("a_xn_done")
        s_x0f, s_x0d = sem("x0_filled"), sem("x0_drained")
        s_x1f, s_x1d = sem("x1_filled"), sem("x1_drained")
        s_khi = sem("k_high")
        s_ksw, s_vhi, s_vsw = sem("keys_switched"), sem("values_high"), sem("values_switched")
        s_qhi = sem("q_high")
        s_qdup = sem("q_high_copied")
        s_s, s_max = sem("scores_for_max"), sem("max_done")
        s_mrow = sem("max_row_placed")
        s_st, s_exp, s_pv = sem("scoresT_done"), sem("exp_done"), sem("pv_done")
        s_xal = sem("xa_low")
        s_lop, s_lod = sem("exp_low_by_pool"), sem("exp_low_by_dve")
        s_oz = sem("head_taken")
        s_zc, s_rc, s_rzd, s_rzb = sem("sums_spread"), sem("reciprocals"), sem("reciprocals_written"), sem("reciprocals_back")
        s_sc = sem("quad_scaled")
        s_out = sem("out_written")

        block = ctx.enter_context(nc.Block())

        X0_START, X0_PER_B = 6, 10
        X1_PER_B = 7

        def x0_use(b, idx):
            return X0_START + X0_PER_B * b + idx

        def x1_use(b, idx):
            return X1_PER_B * b + idx

        def x0_of_q(b, i, ch):
            if i >= 2:
                return x0_use(b, 2 * (i - 2) + ch)
            if isinstance(b, int) and b == 0:
                return 2 + 2 * i + ch
            return x0_use(b - 1, 6 + 2 * i + ch)

        def x0_of_k(b):
            return 0 if isinstance(b, int) and b == 0 else x0_use(b - 1, 4)

        def x0_of_v(b):
            return 1 if isinstance(b, int) and b == 0 else x0_use(b - 1, 5)

        def x1_of_xt(b):
            return 0 if isinstance(b, int) and b == 0 else x1_use(b - 1, 3)

        def x1_of_mt(b, i):
            first, last = (isinstance(b, int) and b == e for e in (0, B - 1))
            if i == 0:
                return 1 if first else x1_use(b - 1, 6)
            return x1_use(b, {1: 2 if first else 0, 2: 3 if last else 4, 3: 4 if last else 5}[i])

        def x1_of_op(b):
            return x1_use(b, 5) if isinstance(b, int) and b == B - 1 else x1_use(b + 1, 1)

        def x1_of_yt(b):
            return x1_use(b, 6) if isinstance(b, int) and b == B - 1 else x1_use(b + 1, 2)

        X1_ALL = X1_PER_B * B
        LAG = 3

        def side_steps(i, n, has_prev, has_next):
            todo = []
            if i or has_prev:
                if n == 6:
                    todo.append(("reciprocals", None))
            if i < 2 or has_next:
                qb, qi = (0, i + 2) if i < 2 else (1, i - 2)
                for ch, steps in ((0, (3, 4, 5, 6, 7)), (1, (8, 9, 10, 11, 15))):
                    if n == steps[0]:
                        todo.append(("q", (qb, qi, ch)))
                    if n == steps[1]:
                        todo.append(("q_high", (qb, qi, ch)))
                    if n in steps[2:4]:
                        todo.append(("q_low", (qb, qi, ch, steps.index(n) - 2)))
                    if n == steps[4]:
                        todo.append(("q_copy", (qb, qi, ch)))
            if i == 1 and has_next:
                todo += {7: [("x_normal", None)], 9: [("x_turn", None)], 10: [("x_turned", None)], 11: [("x_low", None)],
                         13: [("k", None)], 14: [("k_high", None)], 15: [("k_low", None)]}.get(n, [])
            if i == 2 and has_next:
                todo += {0: [("v", None)], 1: [("v_bias", None)]}.get(n, [])
            if i < QUADS - 1 or has_next:
                for k in range(STEPS):
                    if k * 13 // STEPS == n:
                        todo.append(("max", k))
                if n == 13:
                    todo.append(("max_row", None))
            if (i or has_prev) and n in (13, 14):
                todo.append(("scale", n - 13))
            if has_prev and i == 1:
                todo += {0: [("out", 0)], 1: [("out", 1)], 2: [("out", 2)], 3: [("out", 3)],
                         4: [("y_bias", None)], 6: [("y_back", None)], 7: [("add_y", None)]}.get(n, [])
            return todo

        def before(b, i, n, steps):
            if n >= steps:
                return b, i, n - steps
            return (b, i - 1, n - steps + STEPS) if i else (b - 1, QUADS - 1, n - steps + STEPS)

        def bodies(engine, body):
            body(0, False, True)
            with engine.Fori(1, B - 1) as b:
                body(b, True, True)
            body(B - 1, True, False)

        @block.sync
        def _(sp):
            def load_x(b):
                sp.dma_start(xs[:, TPB * b:TPB * (b + 1), :], x[b].rearrange("(j p) d -> p j d", p=P)).then_inc(s_x[b], 16)

            load_x(0)
            for r, a in ((R_B1, b1), (R_B2, b2), (R_B3, b3), (R_BQ, bq.rearrange("(c p) -> c p", p=P)),
                         (R_BO, bo.rearrange("(c p) -> c p", p=P))):
                sp.dma_start(brow[r:r + a.shape[0], :], a).then_inc(s_rows, 16)
            for c in range(2):
                sp.dma_start(brow[R_BK:R_BK + 1, DK * c:DK * (c + 1)], bk.rearrange("(c p) -> c p", p=DK)).then_inc(s_rows, 16)
            for b in range(1, B):
                load_x(b)
            sp.wait_ge(s_zero, 3)
            sp.dma_start(gws[:, 0:E], gate_w).then_inc(s_gb, 16)
            for j in range(TPB):
                sp.dma_start(gbc[SLOT * j:SLOT * j + E, :], gate_b.rearrange("(e c) -> e c", c=1)).then_inc(s_gb, 16)
            for k, a in enumerate((w1, w2, w3)):
                sp.dma_start(wraw[k].rearrange("p (e o) -> p e o", e=E), a.rearrange("e d o -> d e o")).then_inc(s_wf, 16)
            sp.dma_start(wraw[3], Wq).then_inc(s_wf, 16)
            for c in range(2):
                sp.dma_start(wks[:, DK * c:DK * (c + 1)], Wk).then_inc(s_wa, 16)
            sp.dma_start(wvs[:, :], Wv).then_inc(s_wa, 16)
            sp.dma_start(bvb[:, :], bv.partition_broadcast(P)).then_inc(s_wa, 16)

            def weights_out(f):
                s = F[f]
                sp.wait_ge(s["wT_ready"], 2)
                for j in range(TPB):
                    sp.dma_start(wd[:, :, j, :], wT[SLOT * j:SLOT * j + E, :, :]).then_inc(s["wd_written"], 16)
                sp.wait_ge(s["wd_written"], 16 * TPB)
                if f == 0:
                    sp.wait_ge(s_wl, 4)
                    sp.dma_start(wos[:, :, :], Wo.rearrange("(c p) n -> p c n", p=P)).then_inc(s_wa, 16)

                def load_wb(b, slot):
                    sp.dma_start(wbs[slot], wd[:, b, :, :].rearrange("e j p -> e (j p)").partition_broadcast(P)
                                 ).then_inc(s["wb_loaded"], 16)

                load_wb(0, 0)
                sp.wait_ge(s["wb_loaded"], 16)
                sp.wait_ge(s["wsum_done"], 1)
                load_wb(1, 1)
                with sp.Fori(1, B // 2) as c:
                    for slot in range(2):
                        sp.wait_ge(s["l3_bank_free"], 2 + E * (2 * c + slot - 1) + 1)
                        sp.dma_start(wbs[slot], wd[:, bass.ds(2 * c + slot, 1), :, :].rearrange("e o j p -> e (o j p)")
                                     .partition_broadcast(P)).then_inc(s["wb_loaded"], 16)

            def place_max_row(b, i):
                wait(sp, s_x1d, x1_of_mt(b, i) + 1)
                sp.dma_start(QB[DK:DK + 1, i, :, :].rearrange("o h (j s) -> o (h j) s", j=TPB).bitcast(F32), mT.bitcast(F32)).then_inc(s_mrow, 16)

            def send_sums(b, i):
                g = QUADS * b + i
                slot = HPQ * (i % 2)
                wait(sp, s_oz, HPQ * (g + 1))
                for h in range(HPQ):
                    k = 2 * (h % 2) + h // 2
                    row = DK * (1 - h % 2)
                    sp.dma_start(zc[16 * k:16 * (k + 1), :], OZ[row:row + 1, slot + h, :].rearrange("o (q r) -> o q r", q=16)
                                 ).then_inc(s_zc, 16)
                wait(sp, s_rc, g + 1)
                sp.dma_start(rzd[i % 2].rearrange("u h (q r) -> (u h q) r", q=16), rc).then_inc(s_rzd, 16)
                wait(sp, s_rzd, 16 * (g + 1))
                for par in range(2):
                    sp.dma_start(rzb[DK * par:DK * (par + 1), :, :], rzd[i % 2, par].partition_broadcast(DK)).then_inc(s_rzb, 16)

            def attention():
                place_max_row(0, 0)

                def body(b, has_prev, has_next):
                    for i in range(QUADS):
                        if i:
                            send_sums(b, i - 1)
                        elif has_prev:
                            send_sums(b - 1, QUADS - 1)
                        if i + 1 < QUADS:
                            place_max_row(b, i + 1)
                        elif has_next:
                            place_max_row(b + 1, 0)

                bodies(sp, body)
                send_sums(B - 1, QUADS - 1)

            weights_out(0)
            attention()
            weights_out(1)
            for b in range(B):
                sp.wait_ge(F[1]["x_updated"], b + 1)
                sp.dma_start(out[b].rearrange("(j p) d -> p j d", p=P), xs[:, TPB * b:TPB * (b + 1), :]).then_inc(s_out, 16)
            sp.wait_ge(s_out, 16 * B)

        @block.gpsimd
        def _(pool):
            pool.memset(ident[:, :], 0.0).then_inc(s_id0, 1)
            pool.wait_ge(s_id0, 1)
            pool.affine_select(out=ident[:, :], in_=ident[:, :], compare_op=ALU.not_equal, fill=1.0, base=0,
                               pattern=[[-1, P]], channel_multiplier=1).then_inc(s_id, 1)

            def q_copy(b, i, ch):
                wait(pool, s_qhi, 2 * (QUADS * b + i) + ch + 1)
                q = QA[0:DK, i, 2 * ch:2 * ch + 2, :].bitcast(F32)
                one = ones[0:DK, 0:1].unsqueeze(2).to_broadcast([DK, 2, S])
                pool.tensor_tensor(QB[0:DK, i, 2 * ch:2 * ch + 2, :], q, one, ALU.mult).then_inc(s_qdup, 1)

            def exp_low(b, i, n):
                N = STEPS * (QUADS * b + i) + n
                pool.wait_ge(s_exp, N + 1)
                pool.tensor_tensor(Pl[:, n % PD, :], PT[:, n % PD, :], Ph[:, n % PD, :].bitcast(F32), ALU.subtract
                                   ).then_inc(s_lop, 1)

            def xa_low(b):
                wait(pool, s_x1d, x1_of_xt(b) + 1)
                pool.tensor_tensor(XA[:, 1, :], xaT, XA[:, 0, :].bitcast(F32), ALU.subtract).then_inc(s_xal, 1)

            def weights_low():
                for k in range(4):
                    pool.wait_ge(s_wh, k + 1)
                    hi, lo = (wqhi[:, :], wqlo[:, :]) if k == 3 else (
                        t[:, k, :, :].rearrange("p e o -> p (e o)") for t in (whi, wlo))
                    pool.tensor_tensor(lo, wraw[k], hi.bitcast(F32), ALU.subtract).then_inc(s_wl, 1)

            def gate(f):
                s = F[f]
                for b in range(B):
                    pool.wait_ge(s["xnT_ready"], b + 1)
                    pool.tensor_tensor(xl[:, b, :], xnT[:, b, :], xh[:, b, :].bitcast(F32), ALU.subtract).then_inc(s["x_low"], 1)

            def experts(f):
                s = F[f]

                def split2(e, m):
                    pool.wait_ge(s["h2_high"], m + 1)
                    pool.tensor_tensor(h2l[:, e % 2, :], t2[:, e % 2, :], h2h[:, e % 2, :].bitcast(F32), ALU.subtract
                                       ).then_inc(s["h2_ready"], 1)

                def body(b):
                    for e in range(E):
                        split2(e, E * b + e)

                with pool.Fori(0, B) as b:
                    body(b)

            def attention():
                xa_low(0)
                for i in range(2):
                    for ch in range(2):
                        q_copy(0, i, ch)

                def body(b, has_prev, has_next):
                    for i in range(QUADS):
                        for n in range(STEPS):
                            if n % TPB != TPB - 1:
                                exp_low(b, i, n)
                            for stage, arg in side_steps(i, n, has_prev, has_next):
                                if stage == "q_copy":
                                    q_copy(b + arg[0], *arg[1:])
                                elif stage == "x_low":
                                    xa_low(b + 1)

                bodies(pool, body)

            gate(0)
            weights_low()
            experts(0)
            attention()
            gate(1)
            experts(1)

        @block.tensor
        def _(pe):
            pe.wait_ge(s_id, 1)
            pe.wait_ge(s_rows, 16 * 7)
            pe.transpose(psX[0][:, 0:ROWS], brow[:, :], ident[0:ROWS, 0:ROWS]).then_inc(s_bt, 1)

            def gate(f):
                s = F[f]

                def turn_x(b):
                    pe.wait_ge(s["xn_done"], TPB * (b + 1))
                    wait(pe, s["xnT_ready"], b - 1)
                    for j in range(TPB):
                        mm = pe.transpose(psX[b % 2][:, P * j:P * (j + 1)], xn[:, b % 2, j, :], ident[:, :])
                    mm.then_inc(s["xn_transposed"], 1)

                def logits(b):
                    pe.wait_ge(s["xnT_ready"], b + 1)
                    q = b % TPB
                    pe.matmul(psO[b // TPB][SLOT * q:SLOT * (q + 1), :], gws[:, :], xnT[:, b, :], start=True, stop=True
                              ).then_inc(s["logits_done"], 1)

                if f == 0:
                    pe.wait_ge(s_bc, 1)
                    pe.wait_ge(s_gb, 16 * (1 + TPB))
                else:
                    pe.wait_ge(s_x1d, X1_ALL)
                for b in range(B):
                    turn_x(b)
                    if b:
                        logits(b - 1)
                logits(B - 1)
                for g in range(GROUPS):
                    pe.wait_ge(s["probs_ready"], g + 1)
                    if g == 0:
                        pe.wait_ge(s["xnT_ready"], B)
                    for j in range(TPB):
                        mm = pe.transpose(psX[g][:, P * j:P * (j + 1)], prs[:, g, P * j:P * (j + 1)], ident[:, :])
                    mm.then_inc(s["probs_transposed"], 1)
                pe.wait_ge(s["picked"], 1)
                for src, banks in ((indp, psS), (wp, psP)):
                    for b in range(B):
                        q = b % TPB
                        mm = pe.transpose(banks[b // TPB][:, P * q:P * (q + 1)],
                                          src[:, TPB * b:TPB * (b + 1), :].rearrange("p t e -> p (t e)"), ident[:, :])
                        if q == TPB - 1:
                            mm.then_inc(s["picks_transposed"], 1)
                pe.matmul(psX[0][:, 0:NT * E], ones[:, :], wtok[:, :, :].rearrange("p t e -> p (t e)"), start=True, stop=True
                          ).then_inc(s["picks_transposed"], 1)

            def experts(f):
                s = F[f]

                def product(out, layer, e, high, low):
                    pe.matmul(out, whi[:, layer, e, :], high, start=True, stop=False)
                    pe.matmul(out, whi[:, layer, e, :], low, start=False, stop=False)
                    return pe.matmul(out, wlo[:, layer, e, :], high, start=False, stop=True)

                def layer1(e, m, b):
                    wait(pe, s["relu1_done"], m - 1)
                    product(psS[e % 2][:, :], 0, e, xh[:, at(b), :].rearrange("p o s -> p (o s)"),
                            xl[:, at(b), :].rearrange("p o s -> p (o s)")).then_inc(s["l1_done"], 1)

                def layer2(e, m):
                    pe.wait_ge(s["h1_ready"], m + 1)
                    wait(pe, s["relu2_done"], m - 1)
                    product(psP[e % 2][:, :], 1, e, h1h[:, e % 2, :], h1l[:, e % 2, :]).then_inc(s["l2_done"], 1)

                def layer3(e, m):
                    pe.wait_ge(s["h2_ready"], m + 1)
                    pe.wait_ge(s["l3_bank_free"], m + 1)
                    product(psO[e % 2][:, :], 2, e, h2h[:, e % 2, :], h2l[:, e % 2, :]).then_inc(s["l3_done"], 1)

                if f == 0:
                    pe.wait_ge(s_wl, 4)
                pe.wait_ge(s["x_low"], B)
                pe.wait_ge(s["indT_ready"], GROUPS)
                pe.wait_ge(s["wT_ready"], GROUPS)
                layer1(0, 0, 0)
                layer1(1, 1, 0)
                layer2(0, 0)
                layer1(2, 2, 0)
                layer2(1, 1)
                layer1(3, 3, 0)

                def body(b, has_next):
                    for e in range(E):
                        m = E * b + e
                        if e + 4 < E or has_next:
                            layer1((e + 4) % E, m + 4, b if e + 4 < E else b + 1)
                        if e + 2 < E or has_next:
                            layer2((e + 2) % E, m + 2)
                        layer3(e, m)

                body(0, True)
                with pe.Fori(1, B - 1) as b:
                    body(b, True)
                body(B - 1, False)

            def update(f):
                s = F[f]
                pe.wait_ge(s["v_ready"], 1)
                pe.wait_ge(s["wsum_done"], 1)
                pe.transpose(psX[0][:, 0:P], vrep[:, :, :].rearrange("p j e -> p (j e)"), ident[:, :]).then_inc(s["v_transposed"], 1)
                pe.wait_ge(s["VB_ready"], 1)
                for b in range(B):
                    wait(pe, s["x_updated"], b - 1)
                    pe.matmul(psS[b % 2][:, :], indT[:, b, :], VB[:, :, :].rearrange("p j d -> p (j d)"), start=True, stop=True
                              ).then_inc(s["update_done"], 1)

            def x_turn(b):
                pe.wait_ge(s_axn, b + 1)
                wait(pe, s_x1d, x1_of_xt(b))
                for j in range(TPB):
                    mm = pe.transpose(X1[:, P * j:P * (j + 1)], xn[:, 0, j, :], ident[:, :])
                mm.then_inc(s_x1f, 1)

            def k_proj(b):
                wait(pe, s_x1d, x1_of_xt(b) + 1)
                wait(pe, s_x0d, x0_of_k(b))
                pe.matmul(X0[:, :], wks[:, :], xaT, start=True, stop=True).then_inc(s_x0f, 1)

            def v_proj(b):
                wait(pe, s_x0d, x0_of_v(b))
                for j in range(TPB):
                    mm = pe.matmul(X0[:, DK * j:DK * (j + 1)], xaT[:, P * j:P * (j + 1)], wvs[:, :], start=True, stop=True)
                mm.then_inc(s_x0f, 1)

            def q_proj(b, i, ch):
                c = 2 * i + ch
                wait(pe, s_x0d, x0_of_q(b, i, ch))
                if ch == 0:
                    pe.wait_ge(s_xal, b + 1)
                cols = slice(P * c, P * (c + 1))
                pe.matmul(X0[:, :], wqhi[:, cols], XA[:, 0, :], start=True, stop=False)
                pe.matmul(X0[:, :], wqhi[:, cols], XA[:, 1, :], start=False, stop=False)
                pe.matmul(X0[:, :], wqlo[:, cols], XA[:, 0, :], start=False, stop=True).then_inc(s_x0f, 1)

            def scores_for_max(b, i, k):
                g = QUADS * b + i
                if k == 0:
                    wait(pe, s_x0d, x0_of_q(b, i, 1) + 1)
                    if i == 0:
                        pe.wait_ge(s_khi, b + 1)
                wait(pe, s_max, STEPS * g + k - 1)
                h, j = k // TPB, k % TPB
                pe.matmul(psS[k % 2][:, :], QA[:, i, h, P * j:P * (j + 1)], (KAn if i == 0 else KA)[:, :], start=True, stop=True
                          ).then_inc(s_s, 1)

            def turn_max(b, i):
                pe.wait_ge(s_max, STEPS * (QUADS * b + i + 1))
                wait(pe, s_x1d, x1_of_mt(b, i))
                pe.transpose(X1[0:STEPS, 0:P], mx[:, i % 2, :], ident[:, :]).then_inc(s_x1f, 1)

            def scores(b, i, n):
                g = QUADS * b + i
                N = STEPS * g + n
                h, t = n // TPB, n % TPB
                if n == 0:
                    pe.wait_ge(s_mrow, 16 * (g + 1))
                    pe.wait_ge(s_qdup, 2 * (g + 1))
                    if i == 0:
                        pe.wait_ge(s_ksw, b + 1)
                wait(pe, s_exp, N - 1)
                ps = psP[n % 2][:, :]
                pe.matmul(ps, KA[:, P * t:P * (t + 1)], QA[:, i, h, :], start=True, stop=False)
                pe.matmul(ps, KB[:, P * t:P * (t + 1)], QB[:, i, h, :], start=False, stop=True).then_inc(s_st, 1)

            def weigh(b, i, n):
                N = STEPS * (QUADS * b + i) + n
                h, t = n // TPB, n % TPB
                if t == 0:
                    wait(pe, s_oz, HPQ * (QUADS * b + i) + h - 1)
                if n == 0 and i == 0:
                    pe.wait_ge(s_vsw, b + 1)
                if t == TPB - 1:
                    wait(pe, s_lod, HPQ * (QUADS * b + i) + h + 1)
                else:
                    wait(pe, s_lop, (TPB - 1) * (HPQ * (QUADS * b + i) + h) + t + 1)
                vh, vl = (v[:, t, h % 2:h % 2 + 2, :].rearrange("p u d -> p (u d)") for v in (Vh, Vl))
                ps = psO[h % 2][:, :]
                pe.matmul(ps, vh, Ph[:, n % PD, :], start=(t == 0), stop=False)
                pe.matmul(ps, vl, Ph[:, n % PD, :], start=False, stop=False)
                pe.matmul(ps, vh, Pl[:, n % PD, :], start=False, stop=(t == TPB - 1)).then_inc(s_pv, 1)

            def out_proj(b, k):
                if k == 0:
                    wait(pe, s_x1d, x1_of_op(b))
                    pe.wait_ge(s_sc, QUADS * (b + 1))
                for c in (2 * k, 2 * k + 1):
                    mm = pe.matmul(X1[:, :], wos[:, c, :], OT[:, c, :], start=(c == 0), stop=(c == NCH - 1))
                if c == NCH - 1:
                    mm.then_inc(s_x1f, 1)

            def y_back(b):
                wait(pe, s_x1d, x1_of_yt(b))
                for j in range(TPB):
                    mm = pe.transpose(X1[:, P * j:P * (j + 1)], yT[:, P * j:P * (j + 1)], ident[:, :])
                mm.then_inc(s_x1f, 1)

            def attention():
                pe.wait_ge(F[0]["x_updated"], B)
                pe.wait_ge(s_wa, 16 * 5)
                x_turn(0)
                k_proj(0)
                v_proj(0)
                q_proj(0, 0, 0)
                q_proj(0, 0, 1)
                for k in range(STEPS):
                    scores_for_max(0, 0, k)
                    if k % 6 == 2 and k < 12:
                        q_proj(0, 1, k // 6)
                turn_max(0, 0)

                def body(b, has_prev, has_next):
                    for i in range(QUADS):
                        for n in range(STEPS):
                            late = before(b, i, n, LAG) if n >= LAG or i or has_prev else None
                            if late and n == 0:
                                weigh(*late)
                            scores(b, i, n)
                            stages = side_steps(i, n, has_prev, has_next)
                            for stage, arg in stages:
                                nb, ni = (b, i + 1) if i + 1 < QUADS else (b + 1, 0)
                                if stage == "out":
                                    out_proj(b - 1, arg)
                                elif stage == "y_back":
                                    y_back(b - 1)
                                elif stage == "q":
                                    q_proj(b + arg[0], arg[1], arg[2])
                                elif stage == "x_turn":
                                    x_turn(b + 1)
                                elif stage == "k":
                                    k_proj(b + 1)
                                elif stage == "v":
                                    v_proj(b + 1)
                                elif stage == "max":
                                    scores_for_max(nb, ni, arg)
                            if late and n:
                                weigh(*late)
                            if ("max_row", None) in stages:
                                turn_max(nb, ni)

                bodies(pe, body)
                for n in range(STEPS - LAG, STEPS):
                    weigh(B - 1, QUADS - 1, n)
                for k in range(QUADS):
                    out_proj(B - 1, k)
                y_back(B - 1)

            gate(0)
            experts(0)
            update(0)
            attention()
            gate(1)
            experts(1)
            update(1)

        @block.scalar
        def _(act):
            act.wait_ge(s_bt, 1)
            act.copy(bcol[:, :], psX[0][:, 0:ROWS]).then_inc(s_bc, 1)

            def weights_high():
                act.wait_ge(s_wf, 64)
                for k in range(4):
                    dst = wqhi[:, :] if k == 3 else whi[:, k, :, :].rearrange("p e o -> p (e o)")
                    act.copy(dst, wraw[k]).then_inc(s_wh, 1)

            def root(k):
                act.wait_ge(s_var, k + 1)
                act.activation(std[:, :], var[:, :], ACT.Sqrt).then_inc(s_std, 1)

            def gate(f):
                s = F[f]
                for b in range(B):
                    act.wait_ge(s["xn_transposed"], b + 1)
                    act.copy(xh[:, b, :], psX[b % 2][:, :])
                    act.copy(xnT[:, b, :], psX[b % 2][:, :]).then_inc(s["xnT_ready"], 1)
                if f == 0:
                    weights_high()
                for g in range(GROUPS):
                    act.wait_ge(s["logits_biased"], g + 1)
                    act.activation(prs[:, g, :], lgs, ACT.Exp, bias=gst[:, g, 0:1], accum_out=gst[:, g, 1:2]
                                   ).then_inc(s["gate_exp"], 1)
                if f == 0:
                    act.wait_ge(s_wl, 2)
                for g in range(GROUPS):
                    act.wait_ge(s["picks_transposed"], GROUPS + g + 1)
                    act.copy(wT[:, TPB * g:TPB * (g + 1), :].rearrange("p b t -> p (b t)"), psP[g][:, :]).then_inc(s["wT_ready"], 1)

            def experts(f):
                s = F[f]
                if f == 0:
                    act.wait_ge(s_wl, 3)

                def relu1(e, m):
                    act.wait_ge(s["l1_done"], m + 1)
                    wait(act, s["h1_ready"], m - 1)
                    act.activation(t1[:, e % 2, :], psS[e % 2][:, :], ACT.Relu, bias=bcol[:, R_B1 + e:R_B1 + e + 1]
                                   ).then_inc(s["relu1_done"], 1)

                def relu2(e, m):
                    act.wait_ge(s["l2_done"], m + 1)
                    wait(act, s["h2_ready"], m - 1)
                    act.activation(t2[:, e % 2, :], psP[e % 2][:, :], ACT.Relu, bias=bcol[:, R_B2 + e:R_B2 + e + 1]
                                   ).then_inc(s["relu2_done"], 1)
                    wait(act, s["l3_done"], m - 1)
                    act.wait_ge(s["relu2_done"], m + 1)
                    act.copy(h2h[:, e % 2, :], t2[:, e % 2, :]).then_inc(s["h2_high"], 1)

                relu1(0, 0)
                relu1(1, 1)
                relu2(0, 0)
                relu1(2, 2)
                relu2(1, 1)
                relu1(3, 3)

                def body(b, has_next):
                    for e in range(E):
                        m = E * b + e
                        if e + 4 < E or has_next:
                            relu1((e + 4) % E, m + 4)
                        if e + 2 < E or has_next:
                            relu2((e + 2) % E, m + 2)

                body(0, True)
                with act.Fori(1, B - 1) as b:
                    body(b, True)
                body(B - 1, False)

            def x_turned(b):
                wait(act, s_x1f, x1_of_xt(b) + 1)
                if not (isinstance(b, int) and b == 0):
                    act.wait_ge(s_x0f, x0_of_q(b - 1, QUADS - 1, 1) + 1)
                act.copy(XA[:, 0, :], X1[:, :])
                act.copy(xaT, X1[:, :]).then_inc(s_x1d, 1)

            def k_high(b):
                wait(act, s_x0f, x0_of_k(b) + 1)
                wait(act, s_ksw, b)
                if not (isinstance(b, int) and b == 0):
                    act.wait_ge(s_s, STEPS * (QUADS * (b - 1) + 1))
                act.activation(KAn[:, :], X0[:, :], ACT.Identity, bias=bcol[:, R_BK:R_BK + 1]).then_inc(s_khi, 1)

            def q_high(b, i, ch):
                c = 2 * i + ch
                wait(act, s_x0f, x0_of_q(b, i, ch) + 1)
                wait(act, s_st, STEPS * (QUADS * b + i - QUADS + 1))
                for r in range(2):
                    ins = act.activation(QA[0:DK, i, 2 * ch + r, :], X0[DK * r:DK * (r + 1), :], ACT.Identity,
                                         bias=bcol[DK * r:DK * (r + 1), R_BQ + c:R_BQ + c + 1])
                ins.then_inc(s_qhi, 1)

            def exponent(b, i, n):
                N = STEPS * (QUADS * b + i) + n
                act.wait_ge(s_st, N + 1)
                wait(act, s_pv, N - PD + 1)
                act.activation(PT[:, n % PD, :], psP[n % 2][:, :], ACT.Exp, scale=SCALE)
                act.activation(Ph[:, n % PD, :], psP[n % 2][:, :], ACT.Exp, scale=SCALE).then_inc(s_exp, 1)

            def take_head(b, i, h):
                act.wait_ge(s_pv, TPB * (H * b + HPQ * i + h + 1))
                wait(act, s_sc, QUADS * b + i - 1)
                act.copy(OZ[:, HPQ * (i % 2) + h, :], psO[h % 2][:, :]).then_inc(s_oz, 1)

            def y_bias(b):
                wait(act, s_x1f, x1_of_op(b) + 1)
                act.activation(yT, X1[:, :], ACT.Identity, bias=bcol[:, R_BO:R_BO + 1]).then_inc(s_x1d, 1)

            def attention():
                x_turned(0)
                k_high(0)
                for i in range(2):
                    for ch in range(2):
                        q_high(0, i, ch)

                def body(b, has_prev, has_next):
                    for i in range(QUADS):
                        for n in range(STEPS):
                            exponent(b, i, n)
                            for stage, arg in side_steps(i, n, has_prev, has_next):
                                if stage == "q_high":
                                    q_high(b + arg[0], *arg[1:])
                                elif stage == "x_turned":
                                    x_turned(b + 1)
                                elif stage == "k_high":
                                    k_high(b + 1)
                                elif stage == "y_bias":
                                    y_bias(b - 1)
                            if n % TPB == LAG and (n > LAG or i or has_prev):
                                hb, hi, hn = before(b, i, n, LAG + 1)
                                take_head(hb, hi, hn // TPB)

                bodies(act, body)
                take_head(B - 1, QUADS - 1, HPQ - 1)
                y_bias(B - 1)

            root(0)
            gate(0)
            experts(0)
            root(1)
            attention()
            root(2)
            gate(1)
            experts(1)

        @block.vector
        def _(dve):
            for t in (gws, gbc, vrep):
                dve.memset(t[tuple(slice(None) for _ in t.shape)], 0.0)
            dve.memset(ones[:, :], 1.0)
            for e in range(E):
                dve.memset(prio[:, e:e + 1], float(E - e))
            dve.memset(lgs, 0.0)
            dve.memset(prs[0:1, 0, :], -1.0).then_inc(s_zero, 1)
            dve.wait_ge(s_zero, 1)
            dve.tensor_copy(Vh[:, :, 1, :], ones[:, 0:DK].unsqueeze(1).to_broadcast([P, TPB, DK]))
            dve.tensor_copy(Vl[:, :, 1, :], lgs[:, 0:DK].unsqueeze(1).to_broadcast([P, TPB, DK]))
            dve.tensor_copy(KB[DK:P, :], lgs[DK:P, :]).then_inc(s_zero, 1)
            dve.wait_ge(s_zero, 2)
            dve.tensor_copy(KB[DK:DK + 1, :], prs[0:1, 0, :]).then_inc(s_zero, 1)

            ln_count = [0]

            def ln_link(ins):
                ln_count[0] += 1
                ins.then_inc(s_ln, 1)
                dve.wait_ge(s_ln, ln_count[0])

            def tile_stats(b):
                for j in range(TPB):
                    ins = dve.bn_stats(stats[:, at(TPB * b + j), :].rearrange("p o k -> p (o k)"),
                                       xs[:, at(TPB * b + j), :].rearrange("p o d -> p (o d)"))
                return ins

            def finish_stats(k):
                dve.wait_ge(s_stats, k + 1)
                ln_link(dve.tensor_tensor(mean[:, :], stats[:, :, 1], stats[:, :, 4], ALU.add))
                ln_link(dve.tensor_tensor(mdif[:, :], stats[:, :, 1], stats[:, :, 4], ALU.subtract))
                ln_link(dve.tensor_tensor(var[:, :], stats[:, :, 2], stats[:, :, 5], ALU.add))
                ln_link(dve.tensor_tensor(sq[:, :], mdif[:, :], mdif[:, :], ALU.mult))
                ln_link(dve.tensor_scalar(var[:, :], var[:, :], 1.0 / D, EPS, ALU.mult, ALU.add))
                ln_link(dve.tensor_scalar(mean[:, :], mean[:, :], 0.5, None, ALU.mult))
                dve.scalar_tensor_tensor(out=var[:, :], in0=sq[:, :], scalar=0.25, in1=var[:, :], op0=ALU.mult, op1=ALU.add
                                         ).then_inc(s_var, 1)
                dve.wait_ge(s_std, k + 1)
                ln_link(dve.reciprocal(rstd[:, :], std[:, :]))

            def gate(f):
                s = F[f]
                for b in range(B):
                    wait(dve, s["xn_transposed"], b - 1)
                    for j in range(TPB):
                        t = TPB * b + j
                        dve.tensor_scalar(xn[:, b % 2, j, :], xs[:, t, :], mean[:, t:t + 1], rstd[:, t:t + 1],
                                          ALU.subtract, ALU.mult).then_inc(s["xn_done"], 1)
                count = [0]

                def link(ins):
                    count[0] += 1
                    ins.then_inc(s["gate_chain"], 1)
                    dve.wait_ge(s["gate_chain"], count[0])

                dve.memset(indp[:, :, :], 0.0)
                link(dve.memset(wp, 0.0))
                if f == 0:
                    dve.wait_ge(s_gb, 16 * (1 + TPB))
                for g in range(GROUPS):
                    dve.wait_ge(s["logits_done"], TPB * (g + 1))
                    wait(dve, s["gate_exp"], g)
                    link(dve.tensor_scalar(lgs, psO[g][:, :], gbc[:, 0:1], None, ALU.add))
                    dve.tensor_reduce(gst[:, g, 0:1], lgs, AX.X, ALU.max, negate=True).then_inc(s["logits_biased"], 1)
                    dve.wait_ge(s["gate_exp"], g + 1)
                    link(dve.reciprocal(gst[:, g, 2:3], gst[:, g, 1:2]))
                    dve.tensor_scalar(prs[:, g, :], prs[:, g, :], gst[:, g, 2:3], None, ALU.mult).then_inc(s["probs_ready"], 1)
                for g in range(GROUPS):
                    dve.wait_ge(s["probs_transposed"], g + 1)
                    src = psX[g][:, :].rearrange("p (j b e) -> p b j e", j=TPB, b=TPB)[:, :, :, 0:E]
                    dst = pt[:, TPB * TPB * g:TPB * TPB * (g + 1), :].rearrange("p (b j) e -> p b j e", b=TPB)
                    for q in range(TPB):
                        ins = dve.tensor_copy(dst[:, q], src[:, q])
                    link(ins)
                tmb = tm[:, :].unsqueeze(2).to_broadcast([P, NT, E])
                prb = prio[:, :].unsqueeze(1).to_broadcast([P, NT, E])
                for oh, left in ((oh1, pt), (oh2, tb)):
                    link(dve.tensor_reduce(tm[:, :], left, AX.X, ALU.max))
                    link(dve.tensor_tensor(ta, left, tmb, ALU.is_equal))
                    link(dve.tensor_tensor(ta, ta, prb, ALU.mult))
                    link(dve.tensor_reduce(tm[:, :], ta, AX.X, ALU.max))
                    link(dve.tensor_tensor(oh, ta, tmb, ALU.is_equal))
                    if oh is oh1:
                        link(dve.scalar_tensor_tensor(out=tb, in0=oh, scalar=-2.0, in1=pt,
                                                      op0=ALU.mult, op1=ALU.add))
                link(dve.tensor_tensor(indp[:, :, 0:E], oh1, oh2, ALU.add))
                link(dve.tensor_tensor(wtok[:, :, :], indp[:, :, 0:E], pt, ALU.mult))
                dve.tensor_copy(wp[:, :, 0:E], wtok[:, :, :]).then_inc(s["picked"], 1)
                if f == 0:
                    dve.wait_ge(s_wl, 1)
                for g in range(GROUPS):
                    dve.wait_ge(s["picks_transposed"], g + 1)
                    dve.tensor_copy(indT[:, TPB * g:TPB * (g + 1), :].rearrange("p b t -> p (b t)"), psS[g][:, :]
                                    ).then_inc(s["indT_ready"], 1)
                dve.wait_ge(s["picks_transposed"], 2 * GROUPS + 1)
                dve.tensor_reduce(wsum[:, :], psX[0][:, 0:NT * E].rearrange("p (t e) -> p e t", e=E), AX.X, ALU.add
                                  ).then_inc(s["wsum_done"], 1)

            def experts(f):
                s = F[f]
                dve.tensor_scalar(nb3[:, :], bcol[:, R_B3:R_B3 + E], -1.0, None, ALU.mult).then_inc(s["l3_bank_free"], 2)
                dve.wait_ge(s["l3_bank_free"], 2)

                def split1(e, m):
                    dve.wait_ge(s["relu1_done"], m + 1)
                    wait(dve, s["l2_done"], m - 1)
                    dve.tensor_copy(h1h[:, e % 2, :], t1[:, e % 2, :]).then_inc(s["h1_high"], 1)
                    dve.wait_ge(s["h1_high"], m + 1)
                    dve.tensor_tensor(h1l[:, e % 2, :], t1[:, e % 2, :], h1h[:, e % 2, :].bitcast(F32), ALU.subtract
                                      ).then_inc(s["h1_ready"], 1)

                for m in range(4):
                    split1(m, m)

                def body(b, slot, last):
                    dve.wait_ge(s["wb_loaded"], 16 * b + 16)
                    for e in range(E):
                        if e + 4 < E or not last:
                            split1((e + 4) % E, E * b + e + 4)
                        dve.wait_ge(s["l3_done"], E * b + e + 1)
                        z = psO[e % 2][:, :]
                        dve.scalar_tensor_tensor(out=z, in0=z, scalar=nb3[:, e:e + 1], in1=wbs[slot][:, e, :], op0=ALU.max,
                                                 op1=ALU.mult, accum_out=vacc[:, e, at(b)]
                                                 ).then_inc(s["l3_bank_free"], 1)

                body(0, 0, False)
                body(1, 1, False)
                with dve.Fori(1, B // 2 - 1) as c:
                    for slot in range(2):
                        body(2 * c + slot, slot, False)
                body(B - 2, 0, False)
                body(B - 1, 1, True)

            def update(f):
                s = F[f]
                count = [0]

                def link(ins):
                    count[0] += 1
                    ins.then_inc(s["v_chain"], 1)
                    dve.wait_ge(s["v_chain"], count[0])

                dve.wait_ge(s["l3_bank_free"], 2 + B * E)
                dve.wait_ge(s["wsum_done"], 1)
                link(dve.memset(VB, 0.0))
                link(dve.tensor_reduce(vv[:, 0, :], vacc[:, :, :], AX.X, ALU.add))
                link(dve.tensor_tensor(vv[:, 1, :], bcol[:, R_B3:R_B3 + E], wsum[:, :], ALU.mult))
                link(dve.tensor_tensor(vv[:, 0, :], vv[:, 0, :], vv[:, 1, :], ALU.add))
                dve.tensor_scalar(vrep[:, :, 0:E], vv[:, 0:1, :].to_broadcast([P, TPB, E]), 0.5, None, ALU.mult
                                  ).then_inc(s["v_ready"], 1)
                dve.wait_ge(s["v_transposed"], 1)
                for j in range(TPB):
                    ins = dve.tensor_copy(VB[SLOT * j:SLOT * (j + 1), j, :], psX[0][SLOT * j:SLOT * (j + 1), 0:P])
                ins.then_inc(s["VB_ready"], 1)
                for b in range(B):
                    dve.wait_ge(s["update_done"], b + 1)
                    xb = xs[:, TPB * b:TPB * (b + 1), :].rearrange("p j d -> p (j d)")
                    dve.tensor_tensor(xb, xb, psS[b % 2][:, :], ALU.add).then_inc(s["x_updated"], 1)
                    if f == 0:
                        dve.wait_ge(s["x_updated"], b + 1)
                        ins = tile_stats(b)
                if f == 0:
                    ins.then_inc(s_stats, 1)

            def x_normal(b):
                wait(dve, s_x1f, 0 if isinstance(b, int) and b == 0 else x1_of_xt(b - 1) + 1)
                for j in range(TPB):
                    t = at(TPB * b + j)
                    ins = dve.tensor_scalar(xn[:, 0, j, :], xs[:, t, :].rearrange("p o d -> p (o d)"), mean[:, t], rstd[:, t],
                                            ALU.subtract, ALU.mult)
                ins.then_inc(s_axn, 1)

            def k_low(b):
                dve.wait_ge(s_khi, b + 1)
                dve.scalar_tensor_tensor(out=KBn, in0=X0[0:DK, :], scalar=bcol[0:DK, R_BK:R_BK + 1], in1=KAn[0:DK, :],
                                         op0=ALU.add, op1=ALU.subtract).then_inc(s_x0d, 1)

            def v_bias(b):
                wait(dve, s_x0f, x0_of_v(b) + 1)
                wait(dve, s_vsw, b)
                dve.tensor_tensor(Vn, X0[:, 0:TPB * DK].rearrange("p (j d) -> p j d", j=TPB),
                                  bvb[:, :].unsqueeze(1).to_broadcast([P, TPB, DK]), ALU.add).then_inc(s_x0d, 1)

            def q_low(b, i, ch, r):
                c = 2 * i + ch
                wait(dve, s_qhi, 2 * (QUADS * b + i) + ch + 1)
                rows = slice(DK * r, DK * (r + 1))
                ins = dve.scalar_tensor_tensor(out=QA[DK:2 * DK, i, 2 * ch + r, :], in0=X0[rows, :],
                                               scalar=bcol[rows, R_BQ + c:R_BQ + c + 1], in1=QA[0:DK, i, 2 * ch + r, :],
                                               op0=ALU.add, op1=ALU.subtract)
                if r == 1:
                    ins.then_inc(s_x0d, 1)

            def row_max(b, i, k):
                dve.wait_ge(s_s, STEPS * (QUADS * b + i) + k + 1)
                dve.tensor_reduce(mx[:, i % 2, k:k + 1], psS[k % 2][:, :], AX.X, ALU.max).then_inc(s_max, 1)

            def max_turned(b, i):
                wait(dve, s_x1f, x1_of_mt(b, i) + 1)
                wait(dve, s_mrow, 16 * (QUADS * b + i))
                dve.tensor_copy(mT, X1[0:STEPS, 0:P]).then_inc(s_x1d, 1)

            def switch_keys(b):
                wait(dve, s_st, H * TPB * b)
                wait(dve, s_x0d, x0_of_k(b) + 1)
                dve.tensor_copy(KA[:, :], KAn[:, :])
                dve.tensor_copy(KB[0:DK, :], KBn).then_inc(s_ksw, 1)

            def switch_values(b):
                wait(dve, s_pv, H * TPB * b)
                wait(dve, s_x0d, x0_of_v(b) + 1)
                for u in (0, 2):
                    ins = dve.tensor_copy(Vh[:, :, u, :], Vn)
                ins.then_inc(s_vhi, 1)
                dve.wait_ge(s_vhi, b + 1)
                for u in (0, 2):
                    ins = dve.tensor_tensor(Vl[:, :, u, :], Vn, Vh[:, :, u, :].bitcast(F32), ALU.subtract)
                ins.then_inc(s_vsw, 1)

            def exp_low(b, i, n):
                g = QUADS * b + i
                dve.wait_ge(s_exp, STEPS * g + n + 1)
                dve.tensor_tensor(Pl[:, n % PD, :], PT[:, n % PD, :], Ph[:, n % PD, :].bitcast(F32), ALU.subtract
                                  ).then_inc(s_lod, 1)

            def reciprocals(b, i):
                g = QUADS * b + i
                wait(dve, s_zc, 16 * HPQ * (g + 1))
                wait(dve, s_rzd, 16 * g)
                dve.reciprocal(rc, zc).then_inc(s_rc, 1)

            def scale(b, i, par):
                g = QUADS * b + i
                slot = HPQ * (i % 2)
                if par == 0:
                    wait(dve, s_rzb, 32 * (g + 1))
                    if i == 0 and not (isinstance(b, int) and b == 0):
                        dve.wait_ge(s_x1f, x1_of_op(b - 1) + 1)
                rows = slice(DK * par, DK * (par + 1))
                ins = dve.tensor_tensor(OT[rows, 2 * i:2 * i + 2, :], OZ[rows, slot + par:slot + HPQ:2, :], rzb[rows, :, :],
                                        ALU.mult)
                if par == 1:
                    ins.then_inc(s_sc, 1)

            def add_y(b):
                wait(dve, s_x1f, x1_of_yt(b) + 1)
                xb = xs[:, at(TPB * b, TPB), :]
                dve.tensor_tensor(xb, xb, X1[:, :].rearrange("p (j d) -> p j d", j=TPB), ALU.add).then_inc(s_x1d, 1)

            def attention():
                x_normal(0)
                k_low(0)
                v_bias(0)
                for ch in range(2):
                    for r in range(2):
                        q_low(0, 0, ch, r)
                for k in range(STEPS):
                    row_max(0, 0, k)
                    if k % 6 == 4 and k < 12:
                        for r in range(2):
                            q_low(0, 1, k // 6, r)
                    if k == 0:
                        switch_keys(0)
                        switch_values(0)
                max_turned(0, 0)

                def body(b, has_prev, has_next):
                    for i in range(QUADS):
                        for n in range(STEPS):
                            if n % TPB == 0 and (n or i or has_prev):
                                exp_low(*before(b, i, n, 1))
                            if i == 0 and n == LAG and has_prev:
                                switch_values(b)
                            for stage, arg in side_steps(i, n, has_prev, has_next):
                                nb, ni = (b, i + 1) if i + 1 < QUADS else (b + 1, 0)
                                pb, pi = (b, i - 1) if i else (b - 1, QUADS - 1)
                                if stage == "reciprocals":
                                    reciprocals(pb, pi)
                                elif stage == "scale":
                                    scale(pb, pi, arg)
                                elif stage == "add_y":
                                    add_y(b - 1)
                                elif stage == "q_low":
                                    q_low(b + arg[0], *arg[1:])
                                elif stage == "x_normal":
                                    x_normal(b + 1)
                                elif stage == "k_low":
                                    k_low(b + 1)
                                elif stage == "v_bias":
                                    v_bias(b + 1)
                                elif stage == "max":
                                    row_max(nb, ni, arg)
                                elif stage == "max_row":
                                    max_turned(nb, ni)
                                    if i == 1 and has_prev:
                                        tile_stats(b - 1)
                    if has_next:
                        switch_keys(b + 1)

                bodies(dve, body)
                exp_low(B - 1, QUADS - 1, STEPS - 1)
                reciprocals(B - 1, QUADS - 1)
                scale(B - 1, QUADS - 1, 0)
                scale(B - 1, QUADS - 1, 1)
                add_y(B - 1)
                dve.wait_ge(s_x1d, X1_ALL)
                tile_stats(B - 1).then_inc(s_stats, 1)

            for b in range(B):
                dve.wait_ge(s_x[b], 16)
                ins = tile_stats(b)
            ins.then_inc(s_stats, 1)
            finish_stats(0)
            dve.wait_ge(s_bc, 1)
            gate(0)
            experts(0)
            update(0)
            finish_stats(1)
            attention()
            finish_stats(2)
            gate(1)
            experts(1)
            update(1)


_INS = ["L0_attn_x", "L0_attn_Wq", "L0_attn_bq", "L0_attn_Wk", "L0_attn_bk", "L0_attn_Wv", "L0_attn_bv", "L0_attn_Wo",
        "L0_attn_bo", "L0_ffn_gate_w", "L0_ffn_gate_b", "L0_ffn_w1", "L0_ffn_b1", "L0_ffn_w2", "L0_ffn_b2", "L0_ffn_w3",
        "L0_ffn_b3"]


def kernel(**inputs):
    import numpy as _np
    import concourse.bacc as _bacc
    from concourse import mybir as _mybir
    from concourse.bass_utils import run_bass_kernel_spmd as _run

    nc = _bacc.Bacc("TRN2", target_bir_lowering=False, num_devices=1)
    arrays, args = {}, []
    for name in _INS:
        a = _np.ascontiguousarray(inputs[name])
        arrays[f"in_{name}"] = a
        args.append(nc.dram_tensor(f"in_{name}", a.shape, _mybir.dt.from_np(a.dtype), kind="ExternalInput").ap())
    shape = inputs["L0_attn_x"].shape
    args.append(nc.dram_tensor("out_0", shape, _mybir.dt.float32, kind="ExternalOutput").ap())
    macaron_kernel(nc, *args)
    r = _run(nc, [arrays], core_ids=[0])
    return r.results[0]["out_0"]
```

```python
from contextlib import ExitStack

import concourse.bass as bass
from concourse import mybir

F32 = mybir.dt.float32
F32R = mybir.dt.float32r
ALU = mybir.AluOpType
ACT = mybir.ActivationFunctionType
AX = mybir.AxisListType

P = 128
EPS = 1e-5


def wait(engine, semaphore, value):
    if isinstance(value, int) and value <= 0:
        return
    engine.wait_ge(semaphore, value)


def at(start, count=1):
    return slice(start, start + count) if isinstance(start, int) else bass.ds(start, count)


def macaron_kernel(nc, x, Wq, bq, Wk, bk, Wv, bv, Wo, bo, gate_w, gate_b, w1, b1, w2, b2, w3, b3, out):
    B, S, D = x.shape
    E = gate_w.shape[1]
    DK = Wk.shape[1]
    H = Wq.shape[1] // DK
    TPB = S // P
    NT = B * TPB
    NCH = H * DK // P
    SLOT = 32
    GROUPS = B // TPB
    QUADS = H // TPB
    HPQ = H // QUADS
    STEPS = HPQ * TPB
    SCALE = float(DK) ** -0.5
    assert D == P and E == 8 and DK == 64 and TPB == 4 and HPQ == 4

    with ExitStack() as ctx:
        def sb(name, shape, dt=F32):
            return ctx.enter_context(nc.sbuf_tensor(name, shape, dt))

        def bank(name):
            return ctx.enter_context(nc.psum_tensor(name, [P, 512], F32))

        def sem(name):
            return ctx.enter_context(nc.semaphore(name))

        xs = sb("xs", [P, NT, D])
        ident = sb("ident", [P, P])
        ones = sb("ones", [P, P])
        whi = sb("whi", [P, 3, E, P], F32R)
        wlo = sb("wlo", [P, 3, E, P], F32R)
        wqhi = sb("wqhi", [P, H * DK], F32R)
        wqlo = sb("wqlo", [P, H * DK], F32R)
        gws = sb("gws", [P, SLOT])
        wks = sb("wks", [P, 2 * DK])
        wvs = sb("wvs", [P, DK])
        wos = sb("wos", [P, NCH, D])
        R_B1, R_B2, R_B3, R_BQ, R_BO, R_BK, ROWS = 0, E, 2 * E, 3 * E, 3 * E + NCH, 3 * E + NCH + 1, 3 * E + NCH + 2
        bcol = sb("bcol", [P, ROWS])
        nb3 = sb("nb3", [P, E])
        gbc = sb("gbc", [P, 1])
        bvb = sb("bvb", [P, DK])
        prio = sb("prio", [P, E])
        stats = sb("stats", [P, NT, 6])
        mean = sb("mean", [P, NT])
        mdif = sb("mdif", [P, NT])
        var = sb("var", [P, NT])
        sq = sb("sq", [P, NT])
        std = sb("std", [P, NT])
        rstd = sb("rstd", [P, NT])
        xn = sb("xn", [P, 2, TPB, D])
        wb0 = sb("wb_even", [P, E, S], F32R)
        wb1 = sb("wb_odd", [P, E, S])
        wbs = (wb0[:, :, :].bitcast(F32), wb1[:, :, :])
        gst = sb("gst", [P, GROUPS, 4])
        tm = sb("tm", [P, NT])
        indp = sb("indp", [P, NT, SLOT])
        picksT = sb("picksT", [P, 2, B, P])
        indT, wT = (picksT[:, u] for u in range(2))
        t1 = xn[:, :, :, :].rearrange("p u j d -> p u (j d)")
        t2 = sb("t2", [P, 2, S])
        VB = t2[:, 1, :].rearrange("p (j d) -> p j d", j=TPB)
        wraw = [picksT[:, 0, :, :].rearrange("p b t -> p (b t)"), picksT[:, 1, :, :].rearrange("p b t -> p (b t)"),
                t2[:, :, :].rearrange("p u s -> p (u s)"), wos[:, :, :].rearrange("p c n -> p (c n)")]
        vacc = sb("vacc", [P, E, B])
        wsum = sb("wsum", [P, E])
        vv = sb("vv", [P, 2, E])
        vrep = sb("vrep", [P, TPB, SLOT])
        wd = nc.dram_tensor("wd", [E, B, TPB, P], F32, kind="Internal").ap()
        prs = wb1[:, 0:GROUPS, :]
        lgs = wb1[:, 2, :]
        wp = wb1[:, 3:5, :].rearrange("p u s -> p (u s)").rearrange("p (t e) -> p t e", e=SLOT)

        def small(k):
            return wb1[:, 5 + k // 2, 256 * (k % 2):256 * (k % 2 + 1)].rearrange("p (t e) -> p t e", e=E)

        pt, ta, tb, oh1, oh2, wtok = (small(k) for k in range(6))
        brow = wb1[0:ROWS, 4, 0:P]
        QA = sb("QA", [P, QUADS, HPQ, S], F32R)
        QB = sb("QB", [P, QUADS, HPQ, S], F32R)
        XA = sb("XA", [P, 2, S], F32R)
        KA = sb("KA", [P, S], F32R)
        KB = sb("KB", [P, S], F32R)
        KAn = sb("KAn", [P, S], F32R)
        KBn_mT = sb("KBn_mT", [P, S], F32R)
        KBn = KBn_mT[0:DK, :]
        mT = KBn_mT[DK:DK + STEPS, 0:P]
        Vh = sb("Vh", [P, TPB, 3, DK], F32R)
        Vl = sb("Vl", [P, TPB, 3, DK], F32R)
        mx = sb("mx", [P, 2, STEPS])
        rzd = nc.dram_tensor("rzd", [2, 2, 2, S], F32, kind="Internal").ap()
        OT = sb("OT_xnT", [P, NCH, S])
        PT = picksT[:, :, :, :].rearrange("p u b t -> p (u b t)").rearrange("p (n s) -> p n s", s=S)
        PD = 4
        Ph, Pl = wb0[:, 0:PD, :], wb0[:, PD:2 * PD, :]
        xaT = t1[:, 1, :]
        yT = t2[:, 1, :]
        rzb = indp[:, :, :].rearrange("p t e -> p (t e)").rearrange("p (u s) -> p u s", s=S)
        Vn = t2[:, 0, 0:TPB * DK].rearrange("p (j d) -> p j d", j=TPB)
        zc = t2[0:HPQ * 16, 0, TPB * DK:TPB * DK + S // 16]
        rc = t2[0:HPQ * 16, 0, TPB * DK + S // 16:TPB * DK + 2 * S // 16]
        OZ = wb1
        xh = QB[:, 0:2, :, :].rearrange("p u h s -> p (u h) s")
        xl = QB[:, 2:4, :, :].rearrange("p u h s -> p (u h) s")

        def xnT(f, b):
            return PT[:, b % PD, :] if f else OT[:, b, :]

        h1h, h1l, h2h, h2l = (QA[:, k, 0:2, :] for k in range(4))

        psS = [bank("psS0"), bank("psS1")]
        psP = [bank("psP0"), bank("psP1")]
        psO = [bank("psO0"), bank("psO1")]
        X0, X1 = psX = [bank("psX0"), bank("psX1")]
        update_banks = psS + psP + psO

        s_x = [sem(f"x_loaded{b}") for b in range(B)]
        s_wf = sem("split_weights_loaded")
        s_wh = sem("Wq_high")
        s_whd = sem("weights_high_by_dve")
        s_wl = sem("weights_low")
        s_wa = sem("attn_weights_loaded")
        s_wo = sem("Wo_loaded")
        s_rows = sem("bias_rows_loaded")
        s_gb = sem("gate_bias_loaded")
        s_zero = sem("zeroed")
        s_id0 = sem("ident_zeroed")
        s_id = sem("ident_ready")
        s_bt = sem("bias_transposed")
        s_bc = sem("bias_columns")
        s_stats = sem("token_stats")
        s_ln = sem("ln_chain")
        s_var = sem("variance_ready")
        s_std = sem("std_ready")

        def ffn_sems(f):
            names = ("xn_done", "xn_transposed", "xnT_ready", "logits_done", "gate_chain", "logits_biased",
                     "gate_exp", "probs_ready", "probs_transposed", "picked", "picks_transposed", "indT_ready",
                     "wT_ready", "wsum_done", "wd_written", "wb_loaded", "l1_done", "l2_done", "l3_done",
                     "relu1_done", "relu2_done", "l3_bank_free", "h1_high", "h1_ready", "h2_high", "h2_ready",
                     "x_low", "VB_zeroed", "v_chain", "v_ready", "v_transposed",
                     "VB_ready", "update_done", "x_updated")
            return {n: sem(f"f{f}_{n}") for n in names}

        F = [ffn_sems(0), ffn_sems(1)]
        s_wbf = [sem(f"wb_first_loaded{k}") for k in range(E // 2)]
        s_axn = sem("a_xn_done")
        s_x0f, s_x0d = sem("x0_filled"), sem("x0_drained")
        s_x1f, s_x1d = sem("x1_filled"), sem("x1_drained")
        s_khi = sem("k_high")
        s_ksw, s_vhi, s_vsw = sem("keys_switched"), sem("values_high"), sem("values_switched")
        s_qhi = sem("q_high")
        s_qdup = sem("q_high_copied")
        s_s, s_max = sem("scores_for_max"), sem("max_done")
        s_mrow = sem("max_row_placed")
        s_st, s_exp, s_pv = sem("scoresT_done"), sem("exp_done"), sem("pv_done")
        s_xal = sem("xa_low")
        s_lop, s_lod = sem("exp_low_by_pool"), sem("exp_low_by_dve")
        s_oz = sem("head_taken")
        s_zc, s_rc, s_rzd, s_rzb = sem("sums_spread"), sem("reciprocals"), sem("reciprocals_written"), sem("reciprocals_back")
        s_sc = sem("quad_scaled")
        s_out = sem("out_written")
        s_pads = sem("pads_zeroed")
        s_u, s_uc = sem("update_added"), sem("update_copied")

        block = ctx.enter_context(nc.Block())

        X0_START, X0_PER_B = 6, 10
        X1_PER_B = 7

        def x0_use(b, idx):
            return X0_START + X0_PER_B * b + idx

        def x1_use(b, idx):
            return X1_PER_B * b + idx

        def x0_of_q(b, i, ch):
            if i >= 2:
                return x0_use(b, 2 * (i - 2) + ch)
            if isinstance(b, int) and b == 0:
                return 1 + 3 * i + ch
            return x0_use(b - 1, 6 + 2 * i + ch)

        def x0_bank(use):
            if isinstance(use, int) and use < X0_START:
                return (X0, X1, psP[0], psO[1], psP[1], psO[0])[use]
            return X0

        def x0_of_k(b):
            return 0 if isinstance(b, int) and b == 0 else x0_use(b - 1, 4)

        def x0_of_v(b):
            return 3 if isinstance(b, int) and b == 0 else x0_use(b - 1, 5)

        def x1_of_xt(b):
            return 0 if isinstance(b, int) and b == 0 else x1_use(b - 1, 3)

        def x1_of_mt(b, i):
            first, last = (isinstance(b, int) and b == e for e in (0, B - 1))
            if i == 0:
                return 1 if first else x1_use(b - 1, 6)
            return x1_use(b, {1: 2 if first else 0, 2: 3 if last else 4, 3: 4 if last else 5}[i])

        def x1_of_op(b):
            return x1_use(b, 5) if isinstance(b, int) and b == B - 1 else x1_use(b + 1, 1)

        def x1_of_yt(b):
            return x1_use(b, 6) if isinstance(b, int) and b == B - 1 else x1_use(b + 1, 2)

        X1_ALL = X1_PER_B * B
        LAG = 3

        def side_steps(i, n, has_prev, has_next):
            todo = []
            if i or has_prev:
                if n == 6:
                    todo.append(("reciprocals", None))
            if i < 2 or has_next:
                qb, qi = (0, i + 2) if i < 2 else (1, i - 2)
                for ch, steps in ((0, (3, 4, 5, 6, 7)), (1, (7, 8, 9, 10, 15) if i == 1 else (8, 9, 10, 11, 15))):
                    if n == steps[0]:
                        todo.append(("q", (qb, qi, ch)))
                    if n == steps[1]:
                        todo.append(("q_high", (qb, qi, ch)))
                    if n in steps[2:4]:
                        todo.append(("q_low", (qb, qi, ch, steps.index(n) - 2)))
                    if n == steps[4]:
                        todo.append(("q_copy", (qb, qi, ch)))
            if i == 1 and has_next:
                todo += {7: [("x_normal", None)], 9: [("x_turn", None)], 10: [("x_turned", None)], 11: [("x_low", None)],
                         12: [("k", None)], 13: [("k_high", None)], 14: [("k_low", None)]}.get(n, [])
            if i == 2 and has_next:
                todo += {0: [("v", None)], 1: [("v_bias", None)]}.get(n, [])
            if i < QUADS - 1 or has_next:
                for k in range(STEPS):
                    if k * 13 // STEPS == n:
                        todo.append(("max", k))
                if n == 13:
                    todo.append(("max_row", None))
            if i == QUADS - 1 and has_next:
                todo += {13: [("scale", 0)], 15: [("switch_keys", None), ("scale", 1)]}.get(n, [])
            elif (i or has_prev) and n in (13, 14):
                todo.append(("scale", n - 13))
            if has_prev and i == 1:
                todo += {0: [("out", 0)], 1: [("out", 1)], 2: [("out", 2)], 3: [("out", 3)],
                         4: [("y_bias", None)], 6: [("y_back", None)], 7: [("add_y", None)]}.get(n, [])
            if has_prev and i == 2 and n == 3:
                todo.append(("stats", None))
            return todo

        def before(b, i, n, steps):
            if n >= steps:
                return b, i, n - steps
            return (b, i - 1, n - steps + STEPS) if i else (b - 1, QUADS - 1, n - steps + STEPS)

        def gate_steps(f):
            part = [("stats", b) for b in range(TPB)]
            if f == 0:
                return (part + [("moments", 0), ("root", 0)] + [("turn", b) for b in range(TPB)] +
                        [("stats", b) for b in range(TPB, B)] + [("moments", 1), ("root", 1)] +
                        [("turn", TPB), ("turn", TPB + 1), ("bias", 0), ("exp", 0), ("turn", TPB + 2), ("turn", TPB + 3),
                         ("weights", 0), ("weights", 1), ("weights", 2), ("probs", 0), ("bias", 1), ("exp", 1),
                         ("layer1", 0), ("layer1", 1), ("choose", 0), ("picks", 0), ("probs", 1), ("split", 0), ("split", 1),
                         ("layer2", 0), ("layer1", 2), ("layer2", 1), ("layer1", 3), ("choose", 1), ("picks", 1)])
            return ([("moments", 4), ("end_exp_low", None), ("root", 4), ("end_weigh", None), ("end_head", None)] +
                    [("turn", b) for b in range(3)] + [("reciprocals", None)] + [("turn", b) for b in range(3, B - 1)] +
                    [("bias", 0), ("out", (0, 1)), ("exp", 0), ("scale", 0), ("scale", 1), ("probs", 0), ("out", (2, 3)),
                     ("choose", 0), ("y_bias", None), ("y_back", None), ("picks", 0), ("add_y", None),
                     ("stats", B - 1), ("moments", 5), ("root", 5), ("turn", B - 1), ("layer1", 0), ("bias", 1),
                     ("split", 0), ("exp", 1), ("layer1", 1), ("probs", 1), ("split", 1), ("layer2", 0), ("layer1", 2),
                     ("layer2", 1), ("layer1", 3), ("choose", 1), ("picks", 1)])

        PARTS = [slice(0, NT // 2), slice(NT // 2, NT), slice(0, TPB), slice(TPB, NT), slice(0, NT - TPB), slice(NT - TPB, NT)]

        def bodies(engine, body):
            body(0, False, True)
            with engine.Fori(1, B - 1) as b:
                body(b, True, True)
            body(B - 1, True, False)

        @block.sync
        def _(sp):
            def load_x(b):
                sp.dma_start(xs[:, TPB * b:TPB * (b + 1), :], x[b].rearrange("(j p) d -> p j d", p=P)).then_inc(s_x[b], 16)

            for b in range(TPB):
                load_x(b)
            for r, a in ((R_B1, b1), (R_B2, b2), (R_B3, b3), (R_BQ, bq.rearrange("(c p) -> c p", p=P)),
                         (R_BO, bo.rearrange("(c p) -> c p", p=P))):
                sp.dma_start(brow[r:r + a.shape[0], :], a).then_inc(s_rows, 16)
            for c in range(2):
                sp.dma_start(brow[R_BK:R_BK + 1, DK * c:DK * (c + 1)], bk.rearrange("(c p) -> c p", p=DK)).then_inc(s_rows, 16)
            for b in range(TPB, B):
                load_x(b)
            sp.wait_ge(s_zero, 3)
            sp.dma_start(gws[:, 0:E], gate_w).then_inc(s_gb, 16)
            for j in range(TPB):
                sp.dma_start(gbc[SLOT * j:SLOT * j + E, :], gate_b.rearrange("(e c) -> e c", c=1)).then_inc(s_gb, 16)
            for k, a in enumerate((w1, w2, w3)):
                sp.dma_start(wraw[k].rearrange("p (e o) -> p e o", e=E), a.rearrange("e d o -> d e o")).then_inc(s_wf, 16)
            sp.dma_start(wraw[3], Wq).then_inc(s_wf, 16)
            for c in range(2):
                sp.dma_start(wks[:, DK * c:DK * (c + 1)], Wk).then_inc(s_wa, 16)
            sp.dma_start(wvs[:, :], Wv).then_inc(s_wa, 16)
            sp.dma_start(bvb[:, :], bv.partition_broadcast(P)).then_inc(s_wa, 16)

            def weights_out(f):
                s = F[f]
                for g in range(GROUPS):
                    sp.wait_ge(s["wT_ready"], g + 1)
                    for j in range(TPB):
                        sp.dma_start(wd[:, TPB * g:TPB * (g + 1), j, :], wT[SLOT * j:SLOT * j + E, TPB * g:TPB * (g + 1), :]
                                     ).then_inc(s["wd_written"], 16)
                    sp.wait_ge(s["wd_written"], 16 * TPB * (g + 1))
                    if g == 0:
                        for k in range(E // 2):
                            sp.dma_start(wbs[0][:, 2 * k:2 * k + 2, :], wd[2 * k:2 * k + 2, 0, :, :]
                                         .rearrange("e j p -> e (j p)").partition_broadcast(P)).then_inc(s_wbf[k], 16)
                sp.wait_ge(s["wsum_done"], 1)
                sp.dma_start(wbs[1], wd[:, 1, :, :].rearrange("e j p -> e (j p)").partition_broadcast(P)
                             ).then_inc(s["wb_loaded"], 16)
                with sp.Fori(1, B // 2) as c:
                    for slot in range(2):
                        sp.wait_ge(s["l3_bank_free"], 2 + E * (2 * c + slot - 1) + 1)
                        sp.dma_start(wbs[slot], wd[:, bass.ds(2 * c + slot, 1), :, :].rearrange("e o j p -> e (o j p)")
                                     .partition_broadcast(P)).then_inc(s["wb_loaded"], 16)

            def place_max_row(b, i):
                wait(sp, s_x1d, x1_of_mt(b, i) + 1)
                sp.dma_start(QB[DK:DK + 1, i, :, :].rearrange("o h (j s) -> o (h j) s", j=TPB).bitcast(F32),
                             mT.bitcast(F32)).then_inc(s_mrow, 16)

            def send_sums(b, i):
                g = QUADS * b + i
                slot = HPQ * (i % 2)
                wait(sp, s_oz, HPQ * (g + 1))
                for h in range(HPQ):
                    k = 2 * (h % 2) + h // 2
                    row = DK * (1 - h % 2)
                    sp.dma_start(zc[16 * k:16 * (k + 1), :], OZ[row:row + 1, slot + h, :].rearrange("o (q r) -> o q r", q=16)
                                 ).then_inc(s_zc, 16)
                wait(sp, s_rc, g + 1)
                sp.dma_start(rzd[i % 2].rearrange("u h (q r) -> (u h q) r", q=16), rc).then_inc(s_rzd, 16)
                wait(sp, s_rzd, 16 * (g + 1))
                for par in range(2):
                    sp.dma_start(rzb[DK * par:DK * (par + 1), :, :], rzd[i % 2, par].partition_broadcast(DK)).then_inc(s_rzb, 16)

            def attention():
                sp.wait_ge(s_wl, 4)
                sp.dma_start(wos[:, :, :], Wo.rearrange("(c p) n -> p c n", p=P)).then_inc(s_wo, 16)
                place_max_row(0, 0)

                def body(b, has_prev, has_next):
                    for i in range(QUADS):
                        if i:
                            send_sums(b, i - 1)
                        elif has_prev:
                            send_sums(b - 1, QUADS - 1)
                        if i + 1 < QUADS:
                            place_max_row(b, i + 1)
                        elif has_next:
                            place_max_row(b + 1, 0)

                bodies(sp, body)
                send_sums(B - 1, QUADS - 1)

            weights_out(0)
            attention()
            weights_out(1)
            for b in range(B):
                sp.wait_ge(F[1]["x_updated"], b + 1)
                sp.dma_start(out[b].rearrange("(j p) d -> p j d", p=P), xs[:, TPB * b:TPB * (b + 1), :]).then_inc(s_out, 16)
            sp.wait_ge(s_out, 16 * B)

        @block.gpsimd
        def _(pool):
            pool.memset(ident[:, :], 0.0).then_inc(s_id0, 1)
            pool.wait_ge(s_id0, 1)
            pool.affine_select(out=ident[:, :], in_=ident[:, :], compare_op=ALU.not_equal, fill=1.0, base=0,
                               pattern=[[-1, P]], channel_multiplier=1).then_inc(s_id, 1)

            def q_copy(b, i, ch):
                wait(pool, s_qhi, 2 * (QUADS * b + i) + ch + 1)
                q = QA[0:DK, i, 2 * ch:2 * ch + 2, :].bitcast(F32)
                one = ones[0:DK, 0:1].unsqueeze(2).to_broadcast([DK, 2, S])
                pool.tensor_tensor(QB[0:DK, i, 2 * ch:2 * ch + 2, :], q, one, ALU.mult).then_inc(s_qdup, 1)

            def exp_low(b, i, n):
                N = STEPS * (QUADS * b + i) + n
                pool.wait_ge(s_exp, N + 1)
                pool.tensor_tensor(Pl[:, n % PD, :], PT[:, n % PD, :], Ph[:, n % PD, :].bitcast(F32), ALU.subtract
                                   ).then_inc(s_lop, 1)

            def xa_low(b):
                wait(pool, s_x1d, x1_of_xt(b) + 1)
                pool.tensor_tensor(XA[:, 1, :], xaT, XA[:, 0, :].bitcast(F32), ALU.subtract).then_inc(s_xal, 1)

            def weight_low(k):
                if k == 3:
                    pool.wait_ge(s_wh, 1)
                else:
                    pool.wait_ge(s_whd, k + 1)
                hi, lo = (wqhi[:, :], wqlo[:, :]) if k == 3 else (
                    t[:, k, :, :].rearrange("p e o -> p (e o)") for t in (whi, wlo))
                pool.tensor_tensor(lo, wraw[k], hi.bitcast(F32), ALU.subtract).then_inc(s_wl, 1)

            def gate(f):
                s = F[f]
                for stage, arg in gate_steps(f):
                    if stage == "turn":
                        if f == 1 and arg == B - 1:
                            pool.wait_ge(s_sc, QUADS * B)
                            pads()
                        pool.wait_ge(s["xnT_ready"], arg + 1)
                        pool.tensor_tensor(xl[:, arg, :], xnT(f, arg), xh[:, arg, :].bitcast(F32), ALU.subtract
                                           ).then_inc(s["x_low"], 1)
                    elif stage == "weights":
                        weight_low(arg)

            def pads():
                pool.memset(indp[:, :, :], 0.0)
                pool.memset(wp, 0.0).then_inc(s_pads, 1)

            def experts(f):
                s = F[f]

                def split2(e, m):
                    pool.wait_ge(s["h2_high"], m + 1)
                    pool.tensor_tensor(h2l[:, e % 2, :], t2[:, e % 2, :], h2h[:, e % 2, :].bitcast(F32), ALU.subtract
                                       ).then_inc(s["h2_ready"], 1)

                def body(b):
                    for e in range(E):
                        split2(e, E * b + e)

                with pool.Fori(0, B) as b:
                    body(b)
                pool.wait_ge(s["h2_ready"], B * E)
                pool.memset(VB, 0.0).then_inc(s["VB_zeroed"], 1)

            def add_update(b):
                pool.wait_ge(s_uc, b)
                xb = xs[:, TPB * b:TPB * (b + 1), :].rearrange("p j d -> p (j d)")
                pool.tensor_tensor(xb, xb, wb1[:, b - 1, :], ALU.add).then_inc(s_u, 1)

            def attention():
                for b in range(1, TPB - 1):
                    add_update(b)
                xa_low(0)
                for b in range(TPB - 1, B):
                    add_update(b)
                for i in range(2):
                    for ch in range(2):
                        q_copy(0, i, ch)

                def body(b, has_prev, has_next):
                    for i in range(QUADS):
                        for n in range(STEPS):
                            if n % TPB != TPB - 1:
                                exp_low(b, i, n)
                            for stage, arg in side_steps(i, n, has_prev, has_next):
                                if stage == "q_copy":
                                    q_copy(b + arg[0], *arg[1:])
                                elif stage == "x_low":
                                    xa_low(b + 1)

                bodies(pool, body)

            pool.wait_ge(s_bt, 1)
            pads()
            gate(0)
            experts(0)
            weight_low(3)
            attention()
            gate(1)
            experts(1)

        @block.tensor
        def _(pe):
            pe.wait_ge(s_id, 1)
            pe.wait_ge(s_rows, 16 * 7)
            pe.transpose(psP[0][:, 0:ROWS], brow[:, :], ident[0:ROWS, 0:ROWS]).then_inc(s_bt, 1)

            def product(out, layer, e, high, low):
                pe.matmul(out, whi[:, layer, e, :], high, start=True, stop=False)
                pe.matmul(out, whi[:, layer, e, :], low, start=False, stop=False)
                return pe.matmul(out, wlo[:, layer, e, :], high, start=False, stop=True)

            def layer1(s, e, m, b):
                wait(pe, s["relu1_done"], m - 1)
                product(psS[e % 2][:, :], 0, e, xh[:, at(b), :].rearrange("p o s -> p (o s)"),
                        xl[:, at(b), :].rearrange("p o s -> p (o s)")).then_inc(s["l1_done"], 1)

            def layer2(s, e, m):
                pe.wait_ge(s["h1_ready"], m + 1)
                wait(pe, s["relu2_done"], m - 1)
                product(psP[e % 2][:, :], 1, e, h1h[:, e % 2, :], h1l[:, e % 2, :]).then_inc(s["l2_done"], 1)

            def layer3(s, e, m):
                pe.wait_ge(s["h2_ready"], m + 1)
                pe.wait_ge(s["l3_bank_free"], m + 1)
                product(psO[e % 2][:, :], 2, e, h2h[:, e % 2, :], h2l[:, e % 2, :]).then_inc(s["l3_done"], 1)

            def gate(f):
                s = F[f]

                def turn_x(b):
                    pe.wait_ge(s["xn_done"], TPB * (b + 1))
                    wait(pe, s["xnT_ready"], b - 1)
                    for j in range(TPB):
                        mm = pe.transpose(psS[b % 2][:, P * j:P * (j + 1)], xn[:, b % 2, j, :], ident[:, :])
                    mm.then_inc(s["xn_transposed"], 1)

                def logits(b):
                    if f == 0 and b == 0:
                        pe.wait_ge(s_gb, 16 * (1 + TPB))
                    pe.wait_ge(s["xnT_ready"], b + 1)
                    q = b % TPB
                    pe.matmul(psO[b // TPB][SLOT * q:SLOT * (q + 1), :], gws[:, :], xnT(f, b), start=True, stop=True
                              ).then_inc(s["logits_done"], 1)

                pending = None
                for stage, arg in gate_steps(f):
                    if stage == "turn":
                        if f == 1 and arg == 0:
                            pe.wait_ge(s_oz, H * B)
                        turn_x(arg)
                        if pending is not None:
                            logits(pending)
                        pending = arg
                    elif pending is not None and stage in ("bias", "weights", "stats", "reciprocals"):
                        logits(pending)
                        pending = None
                    if stage == "probs":
                        pe.wait_ge(s["probs_ready"], arg + 1)
                        if f == 1 and arg == 1:
                            pe.wait_ge(s_x1d, X1_ALL)
                        for j in range(TPB):
                            mm = pe.transpose(psX[arg][:, P * j:P * (j + 1)], prs[:, arg, P * j:P * (j + 1)], ident[:, :])
                        mm.then_inc(s["probs_transposed"], 1)
                    elif stage == "picks":
                        pe.wait_ge(s["picked"], arg + 1)
                        if arg == 1:
                            pe.wait_ge(s["relu2_done"], 2)
                        elif f == 0:
                            pe.wait_ge(s_bc, 1)
                        for src, bank in ((indp, psX[arg]), (wp, psP[arg])):
                            for q in range(TPB):
                                b = TPB * arg + q
                                mm = pe.transpose(bank[:, P * q:P * (q + 1)],
                                                  src[:, TPB * b:TPB * (b + 1), :].rearrange("p t e -> p (t e)"), ident[:, :])
                            mm.then_inc(s["picks_transposed"], 1)
                    elif stage == "layer1":
                        if arg == 0:
                            pe.wait_ge(s["x_low"], 1)
                            if f == 0:
                                pe.wait_ge(s_wl, 1)
                        if arg < 2:
                            pe.wait_ge(s["xnT_ready"], B - 1 + arg)
                        layer1(s, arg, arg, 0)
                    elif stage == "layer2":
                        if f == 0:
                            pe.wait_ge(s_wl, 2)
                        if arg == 0:
                            pe.wait_ge(s["wT_ready"], 1)
                        layer2(s, arg, arg)
                    elif stage == "end_weigh":
                        for n in range(STEPS - LAG, STEPS):
                            weigh(B - 1, QUADS - 1, n)
                    elif stage == "out":
                        for k in arg:
                            out_proj(B - 1, k)
                    elif stage == "y_back":
                        y_back(B - 1)
                pe.wait_ge(s["indT_ready"], 1)
                pe.matmul(psX[0][:, 0:NT * E], ones[:, :], wtok[:, :, :].rearrange("p t e -> p (t e)"), start=True, stop=True
                          ).then_inc(s["picks_transposed"], 1)

            def experts(f):
                s = F[f]

                if f == 0:
                    pe.wait_ge(s_wl, 3)
                pe.wait_ge(s["x_low"], B)
                pe.wait_ge(s["wT_ready"], GROUPS)

                def body(b, has_next):
                    for e in range(E):
                        m = E * b + e
                        if e + 4 < E or has_next:
                            layer1(s, (e + 4) % E, m + 4, b if e + 4 < E else b + 1)
                        if e + 2 < E or has_next:
                            layer2(s, (e + 2) % E, m + 2)
                        layer3(s, e, m)

                body(0, True)
                with pe.Fori(1, B - 1) as b:
                    body(b, True)
                body(B - 1, False)

            def update(f):
                s = F[f]
                pe.wait_ge(s["v_ready"], 1)
                pe.wait_ge(s["wsum_done"], 1)
                pe.transpose(psX[0][:, 0:P], vrep[:, :, :].rearrange("p j e -> p (j e)"), ident[:, :]).then_inc(s["v_transposed"], 1)
                pe.wait_ge(s["VB_ready"], 1)
                for b in range(B - 3 if f == 0 else B):
                    apply_update(f, b)

            def apply_update(f, b):
                s = F[f]
                bank = update_banks[b % len(update_banks)]
                if f == 0 and b >= len(update_banks):
                    pe.wait_ge(s["x_updated"], 1)
                    wait(pe, s_uc, b - len(update_banks))
                elif f == 1:
                    wait(pe, s["x_updated"], b + 1 - len(update_banks))
                pe.matmul(bank[:, :], indT[:, b, :], VB.rearrange("p j d -> p (j d)"), start=True, stop=True
                          ).then_inc(s["update_done"], 1)

            def x_turn(b):
                pe.wait_ge(s_axn, b + 1)
                wait(pe, s_x1d, x1_of_xt(b))
                for j in range(TPB):
                    mm = pe.transpose(X1[:, P * j:P * (j + 1)], xn[:, 0, j, :], ident[:, :])
                mm.then_inc(s_x1f, 1)

            def k_proj(b):
                wait(pe, s_x1d, x1_of_xt(b) + 1)
                wait(pe, s_x0d, x0_of_k(b))
                pe.matmul(X0[:, :], wks[:, :], xaT, start=True, stop=True).then_inc(s_x0f, 1)

            def v_proj(b):
                bank = x0_bank(x0_of_v(b))
                if bank is X0:
                    wait(pe, s_x0d, x0_of_v(b))
                for j in range(TPB):
                    mm = pe.matmul(bank[:, DK * j:DK * (j + 1)], xaT[:, P * j:P * (j + 1)], wvs[:, :], start=True, stop=True)
                mm.then_inc(s_x0f, 1)

            def q_proj(b, i, ch):
                c = 2 * i + ch
                bank = x0_bank(x0_of_q(b, i, ch))
                if bank is X0:
                    wait(pe, s_x0d, x0_of_q(b, i, ch))
                if ch == 0:
                    pe.wait_ge(s_xal, b + 1)
                cols = slice(P * c, P * (c + 1))
                pe.matmul(bank[:, :], wqhi[:, cols], XA[:, 0, :], start=True, stop=False)
                pe.matmul(bank[:, :], wqhi[:, cols], XA[:, 1, :], start=False, stop=False)
                pe.matmul(bank[:, :], wqlo[:, cols], XA[:, 0, :], start=False, stop=True).then_inc(s_x0f, 1)

            def scores_for_max(b, i, k):
                g = QUADS * b + i
                if k in (0, STEPS // 2):
                    wait(pe, s_x0d, x0_of_q(b, i, 2 * k // STEPS) + 1)
                if k == 0:
                    if i == 0:
                        pe.wait_ge(s_khi, b + 1)
                    elif i == 1:
                        pe.wait_ge(s_ksw, b + 1)
                wait(pe, s_max, STEPS * g + k - 1)
                h, j = k // TPB, k % TPB
                pe.matmul(psS[k % 2][:, :], QA[:, i, h, P * j:P * (j + 1)], (KAn if i == 0 else KA)[:, :], start=True, stop=True
                          ).then_inc(s_s, 1)

            def turn_max(b, i):
                pe.wait_ge(s_max, STEPS * (QUADS * b + i + 1))
                wait(pe, s_x1d, x1_of_mt(b, i))
                pe.transpose(X1[0:STEPS, 0:P], mx[:, i % 2, :], ident[:, :]).then_inc(s_x1f, 1)

            def scores(b, i, n):
                g = QUADS * b + i
                N = STEPS * g + n
                h, t = n // TPB, n % TPB
                if n == 0:
                    pe.wait_ge(s_mrow, 16 * (g + 1))
                    pe.wait_ge(s_qdup, 2 * (g + 1))
                    if i == 0:
                        pe.wait_ge(s_ksw, b + 1)
                wait(pe, s_exp, N - 1)
                ps = psP[n % 2][:, :]
                pe.matmul(ps, KA[:, P * t:P * (t + 1)], QA[:, i, h, :], start=True, stop=False)
                pe.matmul(ps, KB[:, P * t:P * (t + 1)], QB[:, i, h, :], start=False, stop=True).then_inc(s_st, 1)

            def weigh(b, i, n):
                N = STEPS * (QUADS * b + i) + n
                h, t = n // TPB, n % TPB
                if t == 0:
                    wait(pe, s_oz, HPQ * (QUADS * b + i) + h - 1)
                if n == 0 and i == 0:
                    pe.wait_ge(s_vsw, b + 1)
                    if isinstance(b, int) and b == 0:
                        pe.wait_ge(s_x0d, X0_START)
                if t == TPB - 1:
                    wait(pe, s_lod, HPQ * (QUADS * b + i) + h + 1)
                else:
                    wait(pe, s_lop, (TPB - 1) * (HPQ * (QUADS * b + i) + h) + t + 1)
                vh, vl = (v[:, t, h % 2:h % 2 + 2, :].rearrange("p u d -> p (u d)") for v in (Vh, Vl))
                ps = psO[h % 2][:, :]
                pe.matmul(ps, vh, Ph[:, n % PD, :], start=(t == 0), stop=False)
                pe.matmul(ps, vl, Ph[:, n % PD, :], start=False, stop=False)
                pe.matmul(ps, vh, Pl[:, n % PD, :], start=False, stop=(t == TPB - 1)).then_inc(s_pv, 1)

            def out_proj(b, k):
                if k == 0:
                    wait(pe, s_x1d, x1_of_op(b))
                    pe.wait_ge(s_wo, 16)
                pe.wait_ge(s_sc, QUADS * b + k + 1)
                for c in (2 * k, 2 * k + 1):
                    mm = pe.matmul(X1[:, :], wos[:, c, :], OT[:, c, :], start=(c == 0), stop=(c == NCH - 1))
                if c == NCH - 1:
                    mm.then_inc(s_x1f, 1)

            def y_back(b):
                wait(pe, s_x1d, x1_of_yt(b))
                for j in range(TPB):
                    mm = pe.transpose(X1[:, P * j:P * (j + 1)], yT[:, P * j:P * (j + 1)], ident[:, :])
                mm.then_inc(s_x1f, 1)

            def attention():
                pe.wait_ge(s_wa, 16 * 4)
                x_turn(0)
                apply_update(0, B - 3)
                apply_update(0, B - 2)
                k_proj(0)
                apply_update(0, B - 1)
                pe.wait_ge(s_wl, 4)
                q_proj(0, 0, 0)
                pe.wait_ge(s_uc, B - 1)
                q_proj(0, 0, 1)
                for k in range(STEPS):
                    scores_for_max(0, 0, k)
                    if k == 1:
                        q_proj(0, 1, 0)
                    elif k == 3:
                        v_proj(0)
                    elif k == 5:
                        q_proj(0, 1, 1)
                turn_max(0, 0)

                def body(b, has_prev, has_next):
                    for i in range(QUADS):
                        for n in range(STEPS):
                            late = before(b, i, n, LAG) if n >= LAG or i or has_prev else None
                            if late and n == 0:
                                weigh(*late)
                            if n:
                                scores(b, i, n)
                            if n and ("max_row", None) in side_steps(i, n - 1, has_prev, has_next):
                                turn_max(*((b, i + 1) if i + 1 < QUADS else (b + 1, 0)))
                            for stage, arg in side_steps(i, n, has_prev, has_next):
                                nb, ni = (b, i + 1) if i + 1 < QUADS else (b + 1, 0)
                                if stage == "out":
                                    out_proj(b - 1, arg)
                                elif stage == "y_back":
                                    y_back(b - 1)
                                elif stage == "q":
                                    q_proj(b + arg[0], arg[1], arg[2])
                                elif stage == "x_turn":
                                    x_turn(b + 1)
                                elif stage == "k":
                                    k_proj(b + 1)
                                elif stage == "v":
                                    v_proj(b + 1)
                                elif stage == "max":
                                    scores_for_max(nb, ni, arg)
                                    if n == 0 and arg == 0:
                                        scores(b, i, n)
                            if n == 0 and not (i < QUADS - 1 or has_next):
                                scores(b, i, n)
                            if late and n:
                                weigh(*late)

                bodies(pe, body)

            gate(0)
            experts(0)
            update(0)
            attention()
            gate(1)
            experts(1)
            update(1)

        @block.scalar
        def _(act):
            def relu1(s, e, m):
                act.wait_ge(s["l1_done"], m + 1)
                wait(act, s["h1_ready"], m - 1)
                act.activation(t1[:, e % 2, :], psS[e % 2][:, :], ACT.Relu, bias=bcol[:, R_B1 + e:R_B1 + e + 1]
                               ).then_inc(s["relu1_done"], 1)

            def relu2(s, e, m):
                act.wait_ge(s["l2_done"], m + 1)
                wait(act, s["h2_ready"], m - 1)
                act.activation(t2[:, e % 2, :], psP[e % 2][:, :], ACT.Relu, bias=bcol[:, R_B2 + e:R_B2 + e + 1]
                               ).then_inc(s["relu2_done"], 1)
                wait(act, s["l3_done"], m - 1)
                act.wait_ge(s["relu2_done"], m + 1)
                act.copy(h2h[:, e % 2, :], t2[:, e % 2, :]).then_inc(s["h2_high"], 1)

            def wq_high():
                act.copy(wqhi[:, :], wraw[3]).then_inc(s_wh, 1)

            def root(k):
                act.wait_ge(s_var, k + 1)
                act.activation(std[:, PARTS[k]], var[:, PARTS[k]], ACT.Sqrt).then_inc(s_std, 1)

            def gate(f):
                s = F[f]
                for stage, arg in gate_steps(f):
                    if stage == "turn":
                        act.wait_ge(s["xn_transposed"], arg + 1)
                        if f == 1:
                            wait(act, s["x_low"], arg - PD + 1)
                            wait(act, s["logits_done"], arg - PD + 1)
                        act.copy(xh[:, arg, :], psS[arg % 2][:, :])
                        act.copy(xnT(f, arg), psS[arg % 2][:, :]).then_inc(s["xnT_ready"], 1)
                    elif stage == "picks":
                        if f == 0:
                            act.wait_ge(s_wl, 2)
                        else:
                            act.wait_ge(s["x_low"], B - 1 + arg)
                        act.wait_ge(s["picks_transposed"], 2 * arg + 2)
                        act.copy(wT[:, TPB * arg:TPB * (arg + 1), :].rearrange("p b t -> p (b t)"), psP[arg][:, :]
                                 ).then_inc(s["wT_ready"], 1)
                    elif stage == "layer1":
                        if arg == 0:
                            act.wait_ge(s["xn_transposed"], B)
                        relu1(s, arg, arg)
                    elif stage == "layer2":
                        if f == 0 and arg == 0:
                            act.wait_ge(s_wl, 3)
                        relu2(s, arg, arg)
                    elif stage == "root":
                        root(arg)
                        if f == 0 and arg == 0:
                            act.wait_ge(s_bt, 1)
                            act.copy(bcol[:, :], psP[0][:, 0:ROWS]).then_inc(s_bc, 1)
                    elif stage == "exp":
                        act.wait_ge(s["logits_biased"], arg + 1)
                        act.activation(prs[:, arg, :], lgs, ACT.Exp, bias=gst[:, arg, 0:1], accum_out=gst[:, arg, 1:2]
                                       ).then_inc(s["gate_exp"], 1)
                    elif stage == "end_head":
                        take_head(B - 1, QUADS - 1, HPQ - 1)
                    elif stage == "y_bias":
                        y_bias(B - 1)
            def experts(f):
                s = F[f]
                def body(b, has_next):
                    for e in range(E):
                        m = E * b + e
                        if e + 4 < E or has_next:
                            relu1(s, (e + 4) % E, m + 4)
                        if e + 2 < E or has_next:
                            relu2(s, (e + 2) % E, m + 2)

                body(0, True)
                with act.Fori(1, B - 1) as b:
                    body(b, True)
                body(B - 1, False)

            def x_turned(b):
                wait(act, s_x1f, x1_of_xt(b) + 1)
                if not (isinstance(b, int) and b == 0):
                    act.wait_ge(s_x0f, x0_of_q(b - 1, QUADS - 1, 1) + 1)
                act.copy(XA[:, 0, :], X1[:, :])
                act.copy(xaT, X1[:, :]).then_inc(s_x1d, 1)

            def k_high(b):
                wait(act, s_x0f, x0_of_k(b) + 1)
                wait(act, s_ksw, b)
                if not (isinstance(b, int) and b == 0):
                    act.wait_ge(s_s, STEPS * (QUADS * (b - 1) + 1))
                act.activation(KAn[:, :], X0[:, :], ACT.Identity, bias=bcol[:, R_BK:R_BK + 1]).then_inc(s_khi, 1)

            def q_high(b, i, ch):
                c = 2 * i + ch
                wait(act, s_x0f, x0_of_q(b, i, ch) + 1)
                wait(act, s_st, STEPS * (QUADS * b + i - QUADS + 1))
                bank = x0_bank(x0_of_q(b, i, ch))
                for r in range(2):
                    ins = act.activation(QA[0:DK, i, 2 * ch + r, :], bank[DK * r:DK * (r + 1), :], ACT.Identity,
                                         bias=bcol[DK * r:DK * (r + 1), R_BQ + c:R_BQ + c + 1])
                ins.then_inc(s_qhi, 1)

            def exponent(b, i, n):
                N = STEPS * (QUADS * b + i) + n
                act.wait_ge(s_st, N + 1)
                wait(act, s_pv, N - PD + 1)
                act.activation(PT[:, n % PD, :], psP[n % 2][:, :], ACT.Exp, scale=SCALE)
                act.activation(Ph[:, n % PD, :], psP[n % 2][:, :], ACT.Exp, scale=SCALE).then_inc(s_exp, 1)

            def take_head(b, i, h):
                act.wait_ge(s_pv, TPB * (H * b + HPQ * i + h + 1))
                wait(act, s_sc, QUADS * b + i - 1)
                act.copy(OZ[:, HPQ * (i % 2) + h, :], psO[h % 2][:, :]).then_inc(s_oz, 1)

            def y_bias(b):
                wait(act, s_x1f, x1_of_op(b) + 1)
                act.activation(yT, X1[:, :], ACT.Identity, bias=bcol[:, R_BO:R_BO + 1]).then_inc(s_x1d, 1)

            def copy_update(b):
                act.wait_ge(F[0]["update_done"], b + 1)
                act.copy(wb1[:, b - 1, :], update_banks[b % len(update_banks)][:, :]).then_inc(s_uc, 1)

            def attention():
                copy_update(1)
                root(2)
                for b in range(2, B - 3):
                    copy_update(b)
                x_turned(0)
                copy_update(B - 3)
                copy_update(B - 2)
                k_high(0)
                copy_update(B - 1)
                for i in range(2):
                    for ch in range(2):
                        q_high(0, i, ch)
                root(3)

                def body(b, has_prev, has_next):
                    for i in range(QUADS):
                        for n in range(STEPS):
                            exponent(b, i, n)
                            for stage, arg in side_steps(i, n, has_prev, has_next):
                                if stage == "q_high":
                                    q_high(b + arg[0], *arg[1:])
                                elif stage == "x_turned":
                                    x_turned(b + 1)
                                elif stage == "k_high":
                                    k_high(b + 1)
                                elif stage == "y_bias":
                                    y_bias(b - 1)
                            if n % TPB == LAG and (n > LAG or i or has_prev):
                                hb, hi, hn = before(b, i, n, LAG + 1)
                                take_head(hb, hi, hn // TPB)

                bodies(act, body)

            gate(0)
            experts(0)
            wq_high()
            attention()
            gate(1)
            experts(1)

        @block.vector
        def _(dve):
            for t in (gws, gbc, vrep):
                dve.memset(t[tuple(slice(None) for _ in t.shape)], 0.0)
            dve.memset(ones[:, :], 1.0)
            for e in range(E):
                dve.memset(prio[:, e:e + 1], float(E - e))
            dve.memset(lgs, 0.0)
            dve.memset(prs[0:1, 0, :], -1.0).then_inc(s_zero, 1)
            dve.wait_ge(s_zero, 1)
            dve.tensor_copy(Vh[:, :, 1, :], ones[:, 0:DK].unsqueeze(1).to_broadcast([P, TPB, DK]))
            dve.tensor_copy(Vl[:, :, 1, :], lgs[:, 0:DK].unsqueeze(1).to_broadcast([P, TPB, DK]))
            dve.tensor_copy(KB[DK:P, :], lgs[DK:P, :]).then_inc(s_zero, 1)
            dve.wait_ge(s_zero, 2)
            dve.tensor_copy(KB[DK:DK + 1, :], prs[0:1, 0, :]).then_inc(s_zero, 1)

            ln_count = [0]

            def ln_link(ins):
                ln_count[0] += 1
                ins.then_inc(s_ln, 1)
                dve.wait_ge(s_ln, ln_count[0])

            def tile_stats(b):
                for j in range(TPB):
                    ins = dve.bn_stats(stats[:, at(TPB * b + j), :].rearrange("p o k -> p (o k)"),
                                       xs[:, at(TPB * b + j), :].rearrange("p o d -> p (o d)"))
                return ins

            def moments(k):
                t = PARTS[k]
                ln_link(dve.tensor_tensor(mean[:, t], stats[:, t, 1], stats[:, t, 4], ALU.add))
                ln_link(dve.tensor_tensor(mdif[:, t], stats[:, t, 1], stats[:, t, 4], ALU.subtract))
                ln_link(dve.tensor_tensor(var[:, t], stats[:, t, 2], stats[:, t, 5], ALU.add))
                ln_link(dve.tensor_tensor(sq[:, t], mdif[:, t], mdif[:, t], ALU.mult))
                ln_link(dve.tensor_scalar(var[:, t], var[:, t], 1.0 / D, EPS, ALU.mult, ALU.add))
                ln_link(dve.tensor_scalar(mean[:, t], mean[:, t], 0.5, None, ALU.mult))
                dve.scalar_tensor_tensor(out=var[:, t], in0=sq[:, t], scalar=0.25, in1=var[:, t], op0=ALU.mult, op1=ALU.add
                                         ).then_inc(s_var, 1)

            def split1(s, e, m):
                dve.wait_ge(s["relu1_done"], m + 1)
                wait(dve, s["l2_done"], m - 1)
                dve.tensor_copy(h1h[:, e % 2, :], t1[:, e % 2, :]).then_inc(s["h1_high"], 1)
                dve.wait_ge(s["h1_high"], m + 1)
                dve.tensor_tensor(h1l[:, e % 2, :], t1[:, e % 2, :], h1h[:, e % 2, :].bitcast(F32), ALU.subtract
                                  ).then_inc(s["h1_ready"], 1)

            def invert(k):
                dve.wait_ge(s_std, k + 1)
                ln_link(dve.reciprocal(rstd[:, PARTS[k]], std[:, PARTS[k]]))

            def gate(f):
                s = F[f]
                count = [0]

                def link(ins):
                    count[0] += 1
                    ins.then_inc(s["gate_chain"], 1)
                    dve.wait_ge(s["gate_chain"], count[0])

                def normal(b):
                    wait(dve, s["xn_transposed"], b - 1)
                    for j in range(TPB):
                        t = TPB * b + j
                        dve.tensor_scalar(xn[:, b % 2, j, :], xs[:, t, :], mean[:, t:t + 1], rstd[:, t:t + 1],
                                          ALU.subtract, ALU.mult).then_inc(s["xn_done"], 1)

                def bias(g):
                    dve.wait_ge(s["logits_done"], TPB * (g + 1))
                    wait(dve, s["gate_exp"], g)
                    if f == 0 and g == 0:
                        dve.wait_ge(s_gb, 16 * (1 + TPB))
                    link(dve.tensor_scalar(lgs, psO[g][:, :], gbc[:, 0:1], None, ALU.add))
                    dve.tensor_reduce(gst[:, g, 0:1], lgs, AX.X, ALU.max, negate=True).then_inc(s["logits_biased"], 1)

                def probs(g):
                    dve.wait_ge(s["gate_exp"], g + 1)
                    link(dve.reciprocal(gst[:, g, 2:3], gst[:, g, 1:2]))
                    dve.tensor_scalar(prs[:, g, :], prs[:, g, :], gst[:, g, 2:3], None, ALU.mult).then_inc(s["probs_ready"], 1)

                def choose(g):
                    n = TPB * TPB
                    t = slice(n * g, n * (g + 1))
                    dve.wait_ge(s["probs_transposed"], g + 1)
                    src = psX[g][:, :].rearrange("p (j b e) -> p b j e", j=TPB, b=TPB)[:, :, :, 0:E]
                    dst = pt[:, t, :].rearrange("p (b j) e -> p b j e", b=TPB)
                    for q in range(TPB):
                        ins = dve.tensor_copy(dst[:, q], src[:, q])
                    link(ins)
                    tmb = tm[:, t].unsqueeze(2).to_broadcast([P, n, E])
                    prb = prio[:, :].unsqueeze(1).to_broadcast([P, n, E])
                    for oh, left in ((oh1, pt), (oh2, tb)):
                        link(dve.tensor_reduce(tm[:, t], left[:, t, :], AX.X, ALU.max))
                        link(dve.tensor_tensor(ta[:, t, :], left[:, t, :], tmb, ALU.is_equal))
                        link(dve.tensor_tensor(ta[:, t, :], ta[:, t, :], prb, ALU.mult))
                        link(dve.tensor_reduce(tm[:, t], ta[:, t, :], AX.X, ALU.max))
                        link(dve.tensor_tensor(oh[:, t, :], ta[:, t, :], tmb, ALU.is_equal))
                        if oh is oh1:
                            link(dve.scalar_tensor_tensor(out=tb[:, t, :], in0=oh[:, t, :], scalar=-2.0, in1=pt[:, t, :],
                                                          op0=ALU.mult, op1=ALU.add))
                    if g == 0:
                        dve.wait_ge(s_pads, f + 1)
                    link(dve.tensor_tensor(indp[:, t, 0:E], oh1[:, t, :], oh2[:, t, :], ALU.add))
                    link(dve.tensor_tensor(wtok[:, t, :], indp[:, t, 0:E], pt[:, t, :], ALU.mult))
                    dve.tensor_copy(wp[:, t, 0:E], wtok[:, t, :]).then_inc(s["picked"], 1)

                for stage, arg in gate_steps(f):
                    if stage == "stats":
                        if f == 0:
                            dve.wait_ge(s_x[arg], 16)
                        else:
                            dve.wait_ge(s_x1d, X1_ALL)
                        ins = tile_stats(arg)
                    elif stage == "moments":
                        if f == 0 or arg == 5:
                            ins.then_inc(s_stats, 1)
                            dve.wait_ge(s_stats, {0: 1, 1: 2, 5: 5}[arg])
                        elif arg == 4:
                            dve.wait_ge(s_lod, H * B - 1)
                        moments(arg)
                    elif stage == "root":
                        invert(arg)
                    elif stage == "turn":
                        normal(arg)
                    elif stage == "bias":
                        bias(arg)
                    elif stage == "probs":
                        probs(arg)
                    elif stage == "weights":
                        dve.wait_ge(s_wf, 64)
                        dve.tensor_copy(whi[:, arg, :, :].rearrange("p e o -> p (e o)"), wraw[arg]).then_inc(s_whd, 1)
                    elif stage == "split":
                        split1(s, arg, arg)
                    elif stage == "choose":
                        choose(arg)
                    elif stage == "end_exp_low":
                        exp_low(B - 1, QUADS - 1, STEPS - 1)
                    elif stage == "reciprocals":
                        reciprocals(B - 1, QUADS - 1)
                    elif stage == "scale":
                        scale(B - 1, QUADS - 1, arg)
                    elif stage == "add_y":
                        add_y(B - 1)
                if f == 0:
                    dve.wait_ge(s_wl, 1)
                else:
                    dve.wait_ge(s["x_low"], B)
                for g in range(GROUPS):
                    dve.wait_ge(s["picks_transposed"], 2 * g + 1)
                    dve.tensor_copy(indT[:, TPB * g:TPB * (g + 1), :].rearrange("p b t -> p (b t)"), psX[g][:, :]
                                    ).then_inc(s["indT_ready"], 1)
                dve.wait_ge(s["picks_transposed"], 2 * GROUPS + 1)
                dve.tensor_reduce(wsum[:, :], psX[0][:, 0:NT * E].rearrange("p (t e) -> p e t", e=E), AX.X, ALU.add
                                  ).then_inc(s["wsum_done"], 1)

            def experts(f):
                s = F[f]
                if f == 0:
                    dve.wait_ge(s_bc, 1)
                dve.tensor_scalar(nb3[:, :], bcol[:, R_B3:R_B3 + E], -1.0, None, ALU.mult).then_inc(s["l3_bank_free"], 2)
                dve.wait_ge(s["l3_bank_free"], 2)

                for m in range(2, 4):
                    split1(s, m, m)

                def body(b, slot, last):
                    for e in range(E):
                        if e + 4 < E or not last:
                            split1(s, (e + 4) % E, E * b + e + 4)
                        if isinstance(b, int) and b == 0:
                            if e % 2 == 0:
                                dve.wait_ge(s_wbf[e // 2], 16 * (f + 1))
                        elif e == 0:
                            dve.wait_ge(s["wb_loaded"], 16 * b)
                        dve.wait_ge(s["l3_done"], E * b + e + 1)
                        z = psO[e % 2][:, :]
                        dve.scalar_tensor_tensor(out=z, in0=z, scalar=nb3[:, e:e + 1], in1=wbs[slot][:, e, :], op0=ALU.max,
                                                 op1=ALU.mult, accum_out=vacc[:, e, at(b)]
                                                 ).then_inc(s["l3_bank_free"], 1)

                body(0, 0, False)
                body(1, 1, False)
                with dve.Fori(1, B // 2 - 1) as c:
                    for slot in range(2):
                        body(2 * c + slot, slot, False)
                body(B - 2, 0, False)
                body(B - 1, 1, True)

            def update(f):
                s = F[f]
                count = [0]

                def link(ins):
                    count[0] += 1
                    ins.then_inc(s["v_chain"], 1)
                    dve.wait_ge(s["v_chain"], count[0])

                dve.wait_ge(s["l3_bank_free"], 2 + B * E)
                dve.wait_ge(s["wsum_done"], 1)
                link(dve.tensor_reduce(vv[:, 0, :], vacc[:, :, :], AX.X, ALU.add))
                link(dve.tensor_tensor(vv[:, 1, :], bcol[:, R_B3:R_B3 + E], wsum[:, :], ALU.mult))
                link(dve.tensor_tensor(vv[:, 0, :], vv[:, 0, :], vv[:, 1, :], ALU.add))
                dve.tensor_scalar(vrep[:, :, 0:E], vv[:, 0:1, :].to_broadcast([P, TPB, E]), 0.5, None, ALU.mult
                                  ).then_inc(s["v_ready"], 1)
                dve.wait_ge(s["v_transposed"], 1)
                dve.wait_ge(s["VB_zeroed"], 1)
                for j in range(TPB):
                    ins = dve.tensor_copy(VB[SLOT * j:SLOT * (j + 1), j, :], psX[0][SLOT * j:SLOT * (j + 1), 0:P])
                ins.then_inc(s["VB_ready"], 1)
                for b in range(1 if f == 0 else B):
                    dve.wait_ge(s["update_done"], b + 1)
                    xb = xs[:, TPB * b:TPB * (b + 1), :].rearrange("p j d -> p (j d)")
                    dve.tensor_tensor(xb, xb, update_banks[b % len(update_banks)][:, :], ALU.add).then_inc(s["x_updated"], 1)

            def x_normal(b):
                wait(dve, s_x1f, 0 if isinstance(b, int) and b == 0 else x1_of_xt(b - 1) + 1)
                for j in range(TPB):
                    t = at(TPB * b + j)
                    ins = dve.tensor_scalar(xn[:, 0, j, :], xs[:, t, :].rearrange("p o d -> p (o d)"), mean[:, t], rstd[:, t],
                                            ALU.subtract, ALU.mult)
                ins.then_inc(s_axn, 1)

            def k_low(b):
                dve.wait_ge(s_khi, b + 1)
                dve.scalar_tensor_tensor(out=KBn, in0=X0[0:DK, :], scalar=bcol[0:DK, R_BK:R_BK + 1], in1=KAn[0:DK, :],
                                         op0=ALU.add, op1=ALU.subtract).then_inc(s_x0d, 1)

            def v_bias(b):
                wait(dve, s_x0f, x0_of_v(b) + 1)
                wait(dve, s_vsw, b)
                dve.tensor_tensor(Vn, x0_bank(x0_of_v(b))[:, 0:TPB * DK].rearrange("p (j d) -> p j d", j=TPB),
                                  bvb[:, :].unsqueeze(1).to_broadcast([P, TPB, DK]), ALU.add).then_inc(s_x0d, 1)

            def q_low(b, i, ch, r):
                c = 2 * i + ch
                wait(dve, s_qhi, 2 * (QUADS * b + i) + ch + 1)
                rows = slice(DK * r, DK * (r + 1))
                ins = dve.scalar_tensor_tensor(out=QA[DK:2 * DK, i, 2 * ch + r, :], in0=x0_bank(x0_of_q(b, i, ch))[rows, :],
                                               scalar=bcol[rows, R_BQ + c:R_BQ + c + 1], in1=QA[0:DK, i, 2 * ch + r, :],
                                               op0=ALU.add, op1=ALU.subtract)
                if r == 1:
                    ins.then_inc(s_x0d, 1)

            def row_max(b, i, k):
                dve.wait_ge(s_s, STEPS * (QUADS * b + i) + k + 1)
                dve.tensor_reduce(mx[:, i % 2, k:k + 1], psS[k % 2][:, :], AX.X, ALU.max).then_inc(s_max, 1)

            def max_turned(b, i):
                wait(dve, s_x1f, x1_of_mt(b, i) + 1)
                wait(dve, s_mrow, 16 * (QUADS * b + i))
                dve.tensor_copy(mT, X1[0:STEPS, 0:P]).then_inc(s_x1d, 1)

            def switch_keys(b):
                wait(dve, s_st, H * TPB * b)
                wait(dve, s_x0d, x0_of_k(b) + 1)
                dve.tensor_copy(KA[:, :], KAn[:, :])
                dve.tensor_copy(KB[0:DK, :], KBn).then_inc(s_ksw, 1)

            def switch_values(b):
                wait(dve, s_pv, H * TPB * b)
                wait(dve, s_x0d, x0_of_v(b) + 1)
                for u in (0, 2):
                    ins = dve.tensor_copy(Vh[:, :, u, :], Vn)
                ins.then_inc(s_vhi, 1)
                dve.wait_ge(s_vhi, b + 1)
                for u in (0, 2):
                    ins = dve.tensor_tensor(Vl[:, :, u, :], Vn, Vh[:, :, u, :].bitcast(F32), ALU.subtract)
                ins.then_inc(s_vsw, 1)

            def exp_low(b, i, n):
                g = QUADS * b + i
                dve.wait_ge(s_exp, STEPS * g + n + 1)
                dve.tensor_tensor(Pl[:, n % PD, :], PT[:, n % PD, :], Ph[:, n % PD, :].bitcast(F32), ALU.subtract
                                  ).then_inc(s_lod, 1)

            def reciprocals(b, i):
                g = QUADS * b + i
                wait(dve, s_zc, 16 * HPQ * (g + 1))
                wait(dve, s_rzd, 16 * g)
                dve.reciprocal(rc, zc).then_inc(s_rc, 1)

            def scale(b, i, par):
                g = QUADS * b + i
                slot = HPQ * (i % 2)
                if par == 0:
                    wait(dve, s_rzb, 32 * (g + 1))
                    if i == 0 and not (isinstance(b, int) and b == 0):
                        dve.wait_ge(s_x1f, x1_of_op(b - 1) + 1)
                rows = slice(DK * par, DK * (par + 1))
                ins = dve.tensor_tensor(OT[rows, 2 * i:2 * i + 2, :], OZ[rows, slot + par:slot + HPQ:2, :], rzb[rows, :, :],
                                        ALU.mult)
                if par == 1:
                    ins.then_inc(s_sc, 1)

            def add_y(b):
                wait(dve, s_x1f, x1_of_yt(b) + 1)
                xb = xs[:, at(TPB * b, TPB), :]
                dve.tensor_tensor(xb, xb, X1[:, :].rearrange("p (j d) -> p j d", j=TPB), ALU.add).then_inc(s_x1d, 1)

            def attention():
                dve.wait_ge(F[0]["x_updated"], 1)
                tile_stats(0).then_inc(s_stats, 1)
                dve.wait_ge(s_stats, 3)
                moments(2)
                invert(2)
                x_normal(0)

                def updated_stats(b):
                    dve.wait_ge(s_u, b)
                    return tile_stats(b)

                for b in range(1, TPB - 1):
                    updated_stats(b)
                k_low(0)
                updated_stats(TPB - 1)
                updated_stats(TPB)
                for r in range(2):
                    q_low(0, 0, 0, r)
                for k in range(STEPS):
                    row_max(0, 0, k)
                    if k == 1:
                        for r in range(2):
                            q_low(0, 0, 1, r)
                    elif k in (3, 4):
                        updated_stats(TPB + k - 2)
                    elif k == 6:
                        updated_stats(TPB + 3).then_inc(s_stats, 1)
                    elif k == 8:
                        dve.wait_ge(s_stats, 4)
                        moments(3)
                    elif k == 9:
                        v_bias(0)
                max_turned(0, 0)
                switch_keys(0)
                for r in range(2):
                    q_low(0, 1, 0, r)
                invert(3)
                for r in range(2):
                    q_low(0, 1, 1, r)
                switch_values(0)

                def body(b, has_prev, has_next):
                    for i in range(QUADS):
                        for n in range(STEPS):
                            if n % TPB == 0 and (n or i or has_prev):
                                exp_low(*before(b, i, n, 1))
                            if i == 0 and n == LAG and has_prev:
                                switch_values(b)
                            for stage, arg in side_steps(i, n, has_prev, has_next):
                                nb, ni = (b, i + 1) if i + 1 < QUADS else (b + 1, 0)
                                pb, pi = (b, i - 1) if i else (b - 1, QUADS - 1)
                                if stage == "reciprocals":
                                    reciprocals(pb, pi)
                                elif stage == "scale":
                                    scale(pb, pi, arg)
                                elif stage == "add_y":
                                    add_y(b - 1)
                                elif stage == "q_low":
                                    q_low(b + arg[0], *arg[1:])
                                elif stage == "x_normal":
                                    x_normal(b + 1)
                                elif stage == "k_low":
                                    k_low(b + 1)
                                elif stage == "v_bias":
                                    v_bias(b + 1)
                                elif stage == "max":
                                    row_max(nb, ni, arg)
                                elif stage == "max_row":
                                    max_turned(nb, ni)
                                elif stage == "switch_keys":
                                    switch_keys(b + 1)
                                elif stage == "stats":
                                    tile_stats(b - 1)

                bodies(dve, body)

            gate(0)
            experts(0)
            update(0)
            attention()
            gate(1)
            experts(1)
            update(1)


_INS = ["L0_attn_x", "L0_attn_Wq", "L0_attn_bq", "L0_attn_Wk", "L0_attn_bk", "L0_attn_Wv", "L0_attn_bv", "L0_attn_Wo",
        "L0_attn_bo", "L0_ffn_gate_w", "L0_ffn_gate_b", "L0_ffn_w1", "L0_ffn_b1", "L0_ffn_w2", "L0_ffn_b2", "L0_ffn_w3",
        "L0_ffn_b3"]


def kernel(**inputs):
    import numpy as _np
    import concourse.bacc as _bacc
    from concourse import mybir as _mybir
    from concourse.bass_utils import run_bass_kernel_spmd as _run

    nc = _bacc.Bacc("TRN2", target_bir_lowering=False, num_devices=1)
    arrays, args = {}, []
    for name in _INS:
        a = _np.ascontiguousarray(inputs[name])
        arrays[f"in_{name}"] = a
        args.append(nc.dram_tensor(f"in_{name}", a.shape, _mybir.dt.from_np(a.dtype), kind="ExternalInput").ap())
    shape = inputs["L0_attn_x"].shape
    args.append(nc.dram_tensor("out_0", shape, _mybir.dt.float32, kind="ExternalOutput").ap())
    macaron_kernel(nc, *args)
    r = _run(nc, [arrays], core_ids=[0])
    return r.results[0]["out_0"]
```
